# Optimizing a Trainium2 kernel written in Bass

```python
import numpy as np
import jax
import jax.numpy as jnp

def _softmax(x, axis=-1):
    return jax.nn.softmax(x, axis=axis)

def _gelu(x):
    return jax.nn.gelu(x, approximate=True)

def _silu(x):
    return jax.nn.silu(x)

def _sigmoid(x):
    return jax.nn.sigmoid(x)

def _layernorm(x, axis=-1, eps=1e-05):
    m = jnp.mean(x, axis=axis, keepdims=True)
    v = jnp.var(x, axis=axis, keepdims=True)
    return (x - m) / jnp.sqrt(v + eps)

def _scatter_add(tgt, idx, src, axis=0):
    return tgt.at[idx].add(src)

def _segment_sum(src, seg, n):
    return jax.ops.segment_sum(src, seg, n)
kernel_name = 'mk_cond_resid_d4_seqx_r4_036eef'

def setup_inputs(seed: int=0):
    np.random.seed(seed)
    _w = jnp.asarray

    def _rec_inputs():
        import jax
        import jax.numpy as jnp
        _rk = jax.random.key(seed)
        x = -0.0003929 + 0.9999 * jax.random.normal(jax.random.fold_in(_rk, 1), (64, 64, 1024), jnp.float32)
        _lenS = 64 - jax.random.randint(jax.random.fold_in(_rk, 7), (64,), 0, max(1, 64 // 4) + 1, jnp.int32)
        _lenS2 = 64 - jax.random.randint(jax.random.fold_in(_rk, 8), (64,), 0, max(1, 64 // 4) + 1, jnp.int32)
        cond_512 = 0.00782532 + 1.00527 * jax.random.normal(jax.random.fold_in(_rk, 11), (64, 128), jnp.float32)
        return (x, cond_512)
    x, cond_512 = _rec_inputs()

    def _L0_cond_setup():
        import jax, jax.numpy as jnp
        from jax import lax
        import numpy as np
        CIN, COUT, K, STYLE_DIM = (64, 64, 3, 128)
        N_LAYERS = 4
        TYPES = ('same', 'upsample', 'same', 'downsample')
        SCALE = 1.0 / float(np.sqrt(CIN * K ** 2))
        EPS = 1e-08
        _BK = np.array([1.0, 3.0, 3.0, 1.0], dtype=np.float32)
        BLUR_K = _BK / _BK.sum()

        def _blur(x, kern, pad):
            B, C, _ = x.shape
            xp = jnp.pad(x, ((0, 0), (0, 0), (pad[0], pad[1])))
            w = jnp.broadcast_to(kern.astype(x.dtype)[None, None, :], (C, 1, kern.shape[0]))
            return lax.conv_general_dilated(xp, w, (1,), 'VALID', feature_group_count=C, dimension_numbers=('NCH', 'OIH', 'NCH'))

        def _conv_same(x, w):
            p = (K - 1) // 2
            return lax.conv_general_dilated(x[None], w, (1,), [(p, p)], dimension_numbers=('NCH', 'OIH', 'NCH'))[0]

        def _conv_down(x, w):
            return lax.conv_general_dilated(x[None], w, (2,), 'VALID', dimension_numbers=('NCH', 'OIH', 'NCH'))[0]

        def _conv_up(x, w_t):
            return lax.conv_transpose(x[None], w_t, (2,), 'VALID', dimension_numbers=('NCH', 'IOH', 'NCH'), transpose_kernel=True)[0]

        def _layer(x, style, w, b, mw, mb, typ):
            s = style @ mw.T + mb
            weight = SCALE * w * s[:, None, :, None]
            demod = lax.rsqrt(jnp.sum(weight * weight, axis=(2, 3)) + EPS)
            weight = weight * demod[:, :, None, None]
            blur_k = jnp.asarray(BLUR_K)
            if typ == 'same':
                out = jax.vmap(_conv_same)(x, weight) + b[None, :, None]
            elif typ == 'upsample':
                out = jax.vmap(_conv_up)(x, weight.transpose(0, 2, 1, 3)) + b[None, :, None]
                out = _blur(out, 2.0 * blur_k, (1, 1))
            elif typ == 'downsample':
                xb = _blur(x, blur_k, (2, 2))
                out = jax.vmap(_conv_down)(xb, weight) + b[None, :, None]
            else:
                raise NotImplementedError(typ)
            return out
        key = jax.random.key(seed)
        ks = jax.random.split(key, 6)
        B, L = (16, 1024)
        return {'x': jax.random.normal(ks[0], (B, CIN, L), dtype=jnp.float32), 'style': jax.random.normal(ks[1], (B, STYLE_DIM), dtype=jnp.float32), 'weights': jax.random.normal(ks[2], (N_LAYERS, COUT, CIN, K), dtype=jnp.float32), 'biases': jax.random.normal(ks[3], (N_LAYERS, COUT), dtype=jnp.float32) * 0.1, 'mod_w': jax.random.normal(ks[4], (N_LAYERS, CIN, STYLE_DIM), dtype=jnp.float32) / np.sqrt(STYLE_DIM), 'mod_b': 1.0 + 0.1 * jax.random.normal(ks[5], (N_LAYERS, CIN), dtype=jnp.float32)}
    _L0_cond_all = _L0_cond_setup()
    _L0_cond_in = {k: v for k, v in _L0_cond_all.items() if k in ('weights', 'biases', 'mod_w', 'mod_b')}
    del _L0_cond_all

    def _L1_cond_setup():
        import jax, jax.numpy as jnp
        from jax import lax
        import numpy as np
        CIN, COUT, K, STYLE_DIM = (64, 64, 3, 128)
        N_LAYERS = 4
        TYPES = ('same', 'upsample', 'same', 'downsample')
        SCALE = 1.0 / float(np.sqrt(CIN * K ** 2))
        EPS = 1e-08
        _BK = np.array([1.0, 3.0, 3.0, 1.0], dtype=np.float32)
        BLUR_K = _BK / _BK.sum()

        def _blur(x, kern, pad):
            B, C, _ = x.shape
            xp = jnp.pad(x, ((0, 0), (0, 0), (pad[0], pad[1])))
            w = jnp.broadcast_to(kern.astype(x.dtype)[None, None, :], (C, 1, kern.shape[0]))
            return lax.conv_general_dilated(xp, w, (1,), 'VALID', feature_group_count=C, dimension_numbers=('NCH', 'OIH', 'NCH'))

        def _conv_same(x, w):
            p = (K - 1) // 2
            return lax.conv_general_dilated(x[None], w, (1,), [(p, p)], dimension_numbers=('NCH', 'OIH', 'NCH'))[0]

        def _conv_down(x, w):
            return lax.conv_general_dilated(x[None], w, (2,), 'VALID', dimension_numbers=('NCH', 'OIH', 'NCH'))[0]

        def _conv_up(x, w_t):
            return lax.conv_transpose(x[None], w_t, (2,), 'VALID', dimension_numbers=('NCH', 'IOH', 'NCH'), transpose_kernel=True)[0]

        def _layer(x, style, w, b, mw, mb, typ):
            s = style @ mw.T + mb
            weight = SCALE * w * s[:, None, :, None]
            demod = lax.rsqrt(jnp.sum(weight * weight, axis=(2, 3)) + EPS)
            weight = weight * demod[:, :, None, None]
            blur_k = jnp.asarray(BLUR_K)
            if typ == 'same':
                out = jax.vmap(_conv_same)(x, weight) + b[None, :, None]
            elif typ == 'upsample':
                out = jax.vmap(_conv_up)(x, weight.transpose(0, 2, 1, 3)) + b[None, :, None]
                out = _blur(out, 2.0 * blur_k, (1, 1))
            elif typ == 'downsample':
                xb = _blur(x, blur_k, (2, 2))
                out = jax.vmap(_conv_down)(xb, weight) + b[None, :, None]
            else:
                raise NotImplementedError(typ)
            return out
        key = jax.random.key(seed)
        ks = jax.random.split(key, 6)
        B, L = (16, 1024)
        return {'x': jax.random.normal(ks[0], (B, CIN, L), dtype=jnp.float32), 'style': jax.random.normal(ks[1], (B, STYLE_DIM), dtype=jnp.float32), 'weights': jax.random.normal(ks[2], (N_LAYERS, COUT, CIN, K), dtype=jnp.float32), 'biases': jax.random.normal(ks[3], (N_LAYERS, COUT), dtype=jnp.float32) * 0.1, 'mod_w': jax.random.normal(ks[4], (N_LAYERS, CIN, STYLE_DIM), dtype=jnp.float32) / np.sqrt(STYLE_DIM), 'mod_b': 1.0 + 0.1 * jax.random.normal(ks[5], (N_LAYERS, CIN), dtype=jnp.float32)}
    _L1_cond_all = _L1_cond_setup()
    _L1_cond_in = {k: v for k, v in _L1_cond_all.items() if k in ('weights', 'biases', 'mod_w', 'mod_b')}
    del _L1_cond_all

    def _L2_cond_setup():
        import jax, jax.numpy as jnp
        from jax import lax
        import numpy as np
        CIN, COUT, K, STYLE_DIM = (64, 64, 3, 128)
        N_LAYERS = 4
        TYPES = ('same', 'upsample', 'same', 'downsample')
        SCALE = 1.0 / float(np.sqrt(CIN * K ** 2))
        EPS = 1e-08
        _BK = np.array([1.0, 3.0, 3.0, 1.0], dtype=np.float32)
        BLUR_K = _BK / _BK.sum()

        def _blur(x, kern, pad):
            B, C, _ = x.shape
            xp = jnp.pad(x, ((0, 0), (0, 0), (pad[0], pad[1])))
            w = jnp.broadcast_to(kern.astype(x.dtype)[None, None, :], (C, 1, kern.shape[0]))
            return lax.conv_general_dilated(xp, w, (1,), 'VALID', feature_group_count=C, dimension_numbers=('NCH', 'OIH', 'NCH'))

        def _conv_same(x, w):
            p = (K - 1) // 2
            return lax.conv_general_dilated(x[None], w, (1,), [(p, p)], dimension_numbers=('NCH', 'OIH', 'NCH'))[0]

        def _conv_down(x, w):
            return lax.conv_general_dilated(x[None], w, (2,), 'VALID', dimension_numbers=('NCH', 'OIH', 'NCH'))[0]

        def _conv_up(x, w_t):
            return lax.conv_transpose(x[None], w_t, (2,), 'VALID', dimension_numbers=('NCH', 'IOH', 'NCH'), transpose_kernel=True)[0]

        def _layer(x, style, w, b, mw, mb, typ):
            s = style @ mw.T + mb
            weight = SCALE * w * s[:, None, :, None]
            demod = lax.rsqrt(jnp.sum(weight * weight, axis=(2, 3)) + EPS)
            weight = weight * demod[:, :, None, None]
            blur_k = jnp.asarray(BLUR_K)
            if typ == 'same':
                out = jax.vmap(_conv_same)(x, weight) + b[None, :, None]
            elif typ == 'upsample':
                out = jax.vmap(_conv_up)(x, weight.transpose(0, 2, 1, 3)) + b[None, :, None]
                out = _blur(out, 2.0 * blur_k, (1, 1))
            elif typ == 'downsample':
                xb = _blur(x, blur_k, (2, 2))
                out = jax.vmap(_conv_down)(xb, weight) + b[None, :, None]
            else:
                raise NotImplementedError(typ)
            return out
        key = jax.random.key(seed)
        ks = jax.random.split(key, 6)
        B, L = (16, 1024)
        return {'x': jax.random.normal(ks[0], (B, CIN, L), dtype=jnp.float32), 'style': jax.random.normal(ks[1], (B, STYLE_DIM), dtype=jnp.float32), 'weights': jax.random.normal(ks[2], (N_LAYERS, COUT, CIN, K), dtype=jnp.float32), 'biases': jax.random.normal(ks[3], (N_LAYERS, COUT), dtype=jnp.float32) * 0.1, 'mod_w': jax.random.normal(ks[4], (N_LAYERS, CIN, STYLE_DIM), dtype=jnp.float32) / np.sqrt(STYLE_DIM), 'mod_b': 1.0 + 0.1 * jax.random.normal(ks[5], (N_LAYERS, CIN), dtype=jnp.float32)}
    _L2_cond_all = _L2_cond_setup()
    _L2_cond_in = {k: v for k, v in _L2_cond_all.items() if k in ('weights', 'biases', 'mod_w', 'mod_b')}
    del _L2_cond_all

    def _L3_cond_setup():
        import jax, jax.numpy as jnp
        from jax import lax
        import numpy as np
        CIN, COUT, K, STYLE_DIM = (64, 64, 3, 128)
        N_LAYERS = 4
        TYPES = ('same', 'upsample', 'same', 'downsample')
        SCALE = 1.0 / float(np.sqrt(CIN * K ** 2))
        EPS = 1e-08
        _BK = np.array([1.0, 3.0, 3.0, 1.0], dtype=np.float32)
        BLUR_K = _BK / _BK.sum()

        def _blur(x, kern, pad):
            B, C, _ = x.shape
            xp = jnp.pad(x, ((0, 0), (0, 0), (pad[0], pad[1])))
            w = jnp.broadcast_to(kern.astype(x.dtype)[None, None, :], (C, 1, kern.shape[0]))
            return lax.conv_general_dilated(xp, w, (1,), 'VALID', feature_group_count=C, dimension_numbers=('NCH', 'OIH', 'NCH'))

        def _conv_same(x, w):
            p = (K - 1) // 2
            return lax.conv_general_dilated(x[None], w, (1,), [(p, p)], dimension_numbers=('NCH', 'OIH', 'NCH'))[0]

        def _conv_down(x, w):
            return lax.conv_general_dilated(x[None], w, (2,), 'VALID', dimension_numbers=('NCH', 'OIH', 'NCH'))[0]

        def _conv_up(x, w_t):
            return lax.conv_transpose(x[None], w_t, (2,), 'VALID', dimension_numbers=('NCH', 'IOH', 'NCH'), transpose_kernel=True)[0]

        def _layer(x, style, w, b, mw, mb, typ):
            s = style @ mw.T + mb
            weight = SCALE * w * s[:, None, :, None]
            demod = lax.rsqrt(jnp.sum(weight * weight, axis=(2, 3)) + EPS)
            weight = weight * demod[:, :, None, None]
            blur_k = jnp.asarray(BLUR_K)
            if typ == 'same':
                out = jax.vmap(_conv_same)(x, weight) + b[None, :, None]
            elif typ == 'upsample':
                out = jax.vmap(_conv_up)(x, weight.transpose(0, 2, 1, 3)) + b[None, :, None]
                out = _blur(out, 2.0 * blur_k, (1, 1))
            elif typ == 'downsample':
                xb = _blur(x, blur_k, (2, 2))
                out = jax.vmap(_conv_down)(xb, weight) + b[None, :, None]
            else:
                raise NotImplementedError(typ)
            return out
        key = jax.random.key(seed)
        ks = jax.random.split(key, 6)
        B, L = (16, 1024)
        return {'x': jax.random.normal(ks[0], (B, CIN, L), dtype=jnp.float32), 'style': jax.random.normal(ks[1], (B, STYLE_DIM), dtype=jnp.float32), 'weights': jax.random.normal(ks[2], (N_LAYERS, COUT, CIN, K), dtype=jnp.float32), 'biases': jax.random.normal(ks[3], (N_LAYERS, COUT), dtype=jnp.float32) * 0.1, 'mod_w': jax.random.normal(ks[4], (N_LAYERS, CIN, STYLE_DIM), dtype=jnp.float32) / np.sqrt(STYLE_DIM), 'mod_b': 1.0 + 0.1 * jax.random.normal(ks[5], (N_LAYERS, CIN), dtype=jnp.float32)}
    _L3_cond_all = _L3_cond_setup()
    _L3_cond_in = {k: v for k, v in _L3_cond_all.items() if k in ('weights', 'biases', 'mod_w', 'mod_b')}
    del _L3_cond_all
    return {'x': x, 'cond_512': cond_512, 'L0_cond_weights': _L0_cond_in['weights'], 'L0_cond_biases': _L0_cond_in['biases'], 'L0_cond_mod_w': _L0_cond_in['mod_w'], 'L0_cond_mod_b': _L0_cond_in['mod_b'], 'L1_cond_weights': _L1_cond_in['weights'], 'L1_cond_biases': _L1_cond_in['biases'], 'L1_cond_mod_w': _L1_cond_in['mod_w'], 'L1_cond_mod_b': _L1_cond_in['mod_b'], 'L2_cond_weights': _L2_cond_in['weights'], 'L2_cond_biases': _L2_cond_in['biases'], 'L2_cond_mod_w': _L2_cond_in['mod_w'], 'L2_cond_mod_b': _L2_cond_in['mod_b'], 'L3_cond_weights': _L3_cond_in['weights'], 'L3_cond_biases': _L3_cond_in['biases'], 'L3_cond_mod_w': _L3_cond_in['mod_w'], 'L3_cond_mod_b': _L3_cond_in['mod_b']}

def reference(x, cond_512, L0_cond_weights, L0_cond_biases, L0_cond_mod_w, L0_cond_mod_b, L1_cond_weights, L1_cond_biases, L1_cond_mod_w, L1_cond_mod_b, L2_cond_weights, L2_cond_biases, L2_cond_mod_w, L2_cond_mod_b, L3_cond_weights, L3_cond_biases, L3_cond_mod_w, L3_cond_mod_b):
    import jax
    import jax.numpy as jnp

    def _L0_cond_ref(x, style, weights, biases, mod_w, mod_b):
        import jax, jax.numpy as jnp
        from jax import lax
        import numpy as np
        CIN, COUT, K, STYLE_DIM = (64, 64, 3, 128)
        N_LAYERS = 4
        TYPES = ('same', 'upsample', 'same', 'downsample')
        SCALE = 1.0 / float(np.sqrt(CIN * K ** 2))
        EPS = 1e-08
        _BK = np.array([1.0, 3.0, 3.0, 1.0], dtype=np.float32)
        BLUR_K = _BK / _BK.sum()

        def _blur(x, kern, pad):
            B, C, _ = x.shape
            xp = jnp.pad(x, ((0, 0), (0, 0), (pad[0], pad[1])))
            w = jnp.broadcast_to(kern.astype(x.dtype)[None, None, :], (C, 1, kern.shape[0]))
            return lax.conv_general_dilated(xp, w, (1,), 'VALID', feature_group_count=C, dimension_numbers=('NCH', 'OIH', 'NCH'))

        def _conv_same(x, w):
            p = (K - 1) // 2
            return lax.conv_general_dilated(x[None], w, (1,), [(p, p)], dimension_numbers=('NCH', 'OIH', 'NCH'))[0]

        def _conv_down(x, w):
            return lax.conv_general_dilated(x[None], w, (2,), 'VALID', dimension_numbers=('NCH', 'OIH', 'NCH'))[0]

        def _conv_up(x, w_t):
            return lax.conv_transpose(x[None], w_t, (2,), 'VALID', dimension_numbers=('NCH', 'IOH', 'NCH'), transpose_kernel=True)[0]

        def _layer(x, style, w, b, mw, mb, typ):
            s = style @ mw.T + mb
            weight = SCALE * w * s[:, None, :, None]
            demod = lax.rsqrt(jnp.sum(weight * weight, axis=(2, 3)) + EPS)
            weight = weight * demod[:, :, None, None]
            blur_k = jnp.asarray(BLUR_K)
            if typ == 'same':
                out = jax.vmap(_conv_same)(x, weight) + b[None, :, None]
            elif typ == 'upsample':
                out = jax.vmap(_conv_up)(x, weight.transpose(0, 2, 1, 3)) + b[None, :, None]
                out = _blur(out, 2.0 * blur_k, (1, 1))
            elif typ == 'downsample':
                xb = _blur(x, blur_k, (2, 2))
                out = jax.vmap(_conv_down)(xb, weight) + b[None, :, None]
            else:
                raise NotImplementedError(typ)
            return out
        out = x
        for i, typ in enumerate(TYPES):
            out = _layer(out, style, weights[i], biases[i], mod_w[i], mod_b[i], typ)
        return out

    def _L1_cond_ref(x, style, weights, biases, mod_w, mod_b):
        import jax, jax.numpy as jnp
        from jax import lax
        import numpy as np
        CIN, COUT, K, STYLE_DIM = (64, 64, 3, 128)
        N_LAYERS = 4
        TYPES = ('same', 'upsample', 'same', 'downsample')
        SCALE = 1.0 / float(np.sqrt(CIN * K ** 2))
        EPS = 1e-08
        _BK = np.array([1.0, 3.0, 3.0, 1.0], dtype=np.float32)
        BLUR_K = _BK / _BK.sum()

        def _blur(x, kern, pad):
            B, C, _ = x.shape
            xp = jnp.pad(x, ((0, 0), (0, 0), (pad[0], pad[1])))
            w = jnp.broadcast_to(kern.astype(x.dtype)[None, None, :], (C, 1, kern.shape[0]))
            return lax.conv_general_dilated(xp, w, (1,), 'VALID', feature_group_count=C, dimension_numbers=('NCH', 'OIH', 'NCH'))

        def _conv_same(x, w):
            p = (K - 1) // 2
            return lax.conv_general_dilated(x[None], w, (1,), [(p, p)], dimension_numbers=('NCH', 'OIH', 'NCH'))[0]

        def _conv_down(x, w):
            return lax.conv_general_dilated(x[None], w, (2,), 'VALID', dimension_numbers=('NCH', 'OIH', 'NCH'))[0]

        def _conv_up(x, w_t):
            return lax.conv_transpose(x[None], w_t, (2,), 'VALID', dimension_numbers=('NCH', 'IOH', 'NCH'), transpose_kernel=True)[0]

        def _layer(x, style, w, b, mw, mb, typ):
            s = style @ mw.T + mb
            weight = SCALE * w * s[:, None, :, None]
            demod = lax.rsqrt(jnp.sum(weight * weight, axis=(2, 3)) + EPS)
            weight = weight * demod[:, :, None, None]
            blur_k = jnp.asarray(BLUR_K)
            if typ == 'same':
                out = jax.vmap(_conv_same)(x, weight) + b[None, :, None]
            elif typ == 'upsample':
                out = jax.vmap(_conv_up)(x, weight.transpose(0, 2, 1, 3)) + b[None, :, None]
                out = _blur(out, 2.0 * blur_k, (1, 1))
            elif typ == 'downsample':
                xb = _blur(x, blur_k, (2, 2))
                out = jax.vmap(_conv_down)(xb, weight) + b[None, :, None]
            else:
                raise NotImplementedError(typ)
            return out
        out = x
        for i, typ in enumerate(TYPES):
            out = _layer(out, style, weights[i], biases[i], mod_w[i], mod_b[i], typ)
        return out

    def _L2_cond_ref(x, style, weights, biases, mod_w, mod_b):
        import jax, jax.numpy as jnp
        from jax import lax
        import numpy as np
        CIN, COUT, K, STYLE_DIM = (64, 64, 3, 128)
        N_LAYERS = 4
        TYPES = ('same', 'upsample', 'same', 'downsample')
        SCALE = 1.0 / float(np.sqrt(CIN * K ** 2))
        EPS = 1e-08
        _BK = np.array([1.0, 3.0, 3.0, 1.0], dtype=np.float32)
        BLUR_K = _BK / _BK.sum()

        def _blur(x, kern, pad):
            B, C, _ = x.shape
            xp = jnp.pad(x, ((0, 0), (0, 0), (pad[0], pad[1])))
            w = jnp.broadcast_to(kern.astype(x.dtype)[None, None, :], (C, 1, kern.shape[0]))
            return lax.conv_general_dilated(xp, w, (1,), 'VALID', feature_group_count=C, dimension_numbers=('NCH', 'OIH', 'NCH'))

        def _conv_same(x, w):
            p = (K - 1) // 2
            return lax.conv_general_dilated(x[None], w, (1,), [(p, p)], dimension_numbers=('NCH', 'OIH', 'NCH'))[0]

        def _conv_down(x, w):
            return lax.conv_general_dilated(x[None], w, (2,), 'VALID', dimension_numbers=('NCH', 'OIH', 'NCH'))[0]

        def _conv_up(x, w_t):
            return lax.conv_transpose(x[None], w_t, (2,), 'VALID', dimension_numbers=('NCH', 'IOH', 'NCH'), transpose_kernel=True)[0]

        def _layer(x, style, w, b, mw, mb, typ):
            s = style @ mw.T + mb
            weight = SCALE * w * s[:, None, :, None]
            demod = lax.rsqrt(jnp.sum(weight * weight, axis=(2, 3)) + EPS)
            weight = weight * demod[:, :, None, None]
            blur_k = jnp.asarray(BLUR_K)
            if typ == 'same':
                out = jax.vmap(_conv_same)(x, weight) + b[None, :, None]
            elif typ == 'upsample':
                out = jax.vmap(_conv_up)(x, weight.transpose(0, 2, 1, 3)) + b[None, :, None]
                out = _blur(out, 2.0 * blur_k, (1, 1))
            elif typ == 'downsample':
                xb = _blur(x, blur_k, (2, 2))
                out = jax.vmap(_conv_down)(xb, weight) + b[None, :, None]
            else:
                raise NotImplementedError(typ)
            return out
        out = x
        for i, typ in enumerate(TYPES):
            out = _layer(out, style, weights[i], biases[i], mod_w[i], mod_b[i], typ)
        return out

    def _L3_cond_ref(x, style, weights, biases, mod_w, mod_b):
        import jax, jax.numpy as jnp
        from jax import lax
        import numpy as np
        CIN, COUT, K, STYLE_DIM = (64, 64, 3, 128)
        N_LAYERS = 4
        TYPES = ('same', 'upsample', 'same', 'downsample')
        SCALE = 1.0 / float(np.sqrt(CIN * K ** 2))
        EPS = 1e-08
        _BK = np.array([1.0, 3.0, 3.0, 1.0], dtype=np.float32)
        BLUR_K = _BK / _BK.sum()

        def _blur(x, kern, pad):
            B, C, _ = x.shape
            xp = jnp.pad(x, ((0, 0), (0, 0), (pad[0], pad[1])))
            w = jnp.broadcast_to(kern.astype(x.dtype)[None, None, :], (C, 1, kern.shape[0]))
            return lax.conv_general_dilated(xp, w, (1,), 'VALID', feature_group_count=C, dimension_numbers=('NCH', 'OIH', 'NCH'))

        def _conv_same(x, w):
            p = (K - 1) // 2
            return lax.conv_general_dilated(x[None], w, (1,), [(p, p)], dimension_numbers=('NCH', 'OIH', 'NCH'))[0]

        def _conv_down(x, w):
            return lax.conv_general_dilated(x[None], w, (2,), 'VALID', dimension_numbers=('NCH', 'OIH', 'NCH'))[0]

        def _conv_up(x, w_t):
            return lax.conv_transpose(x[None], w_t, (2,), 'VALID', dimension_numbers=('NCH', 'IOH', 'NCH'), transpose_kernel=True)[0]

        def _layer(x, style, w, b, mw, mb, typ):
            s = style @ mw.T + mb
            weight = SCALE * w * s[:, None, :, None]
            demod = lax.rsqrt(jnp.sum(weight * weight, axis=(2, 3)) + EPS)
            weight = weight * demod[:, :, None, None]
            blur_k = jnp.asarray(BLUR_K)
            if typ == 'same':
                out = jax.vmap(_conv_same)(x, weight) + b[None, :, None]
            elif typ == 'upsample':
                out = jax.vmap(_conv_up)(x, weight.transpose(0, 2, 1, 3)) + b[None, :, None]
                out = _blur(out, 2.0 * blur_k, (1, 1))
            elif typ == 'downsample':
                xb = _blur(x, blur_k, (2, 2))
                out = jax.vmap(_conv_down)(xb, weight) + b[None, :, None]
            else:
                raise NotImplementedError(typ)
            return out
        out = x
        for i, typ in enumerate(TYPES):
            out = _layer(out, style, weights[i], biases[i], mod_w[i], mod_b[i], typ)
        return out
    x = x + _L0_cond_ref(x, cond_512, L0_cond_weights, L0_cond_biases, L0_cond_mod_w, L0_cond_mod_b)
    x = x + _L1_cond_ref(x, cond_512, L1_cond_weights, L1_cond_biases, L1_cond_mod_w, L1_cond_mod_b)
    x = x + _L2_cond_ref(x, cond_512, L2_cond_weights, L2_cond_biases, L2_cond_mod_w, L2_cond_mod_b)
    x = x + _L3_cond_ref(x, cond_512, L3_cond_weights, L3_cond_biases, L3_cond_mod_w, L3_cond_mod_b)
    return x

_drawn_inputs = setup_inputs


def setup_inputs(seed=0):
    import zlib

    import numpy as np

    out = dict(_drawn_inputs(seed))
    spreads = {}
    factors = {}
    for name, (base, spread) in spreads.items():
        noise = np.random.default_rng([zlib.crc32(name.encode()), seed]).standard_normal(out[name].shape)
        drawn = base * np.exp(spread * noise) if base else spread * noise
        out[name] = jnp.asarray(drawn.astype(out[name].dtype))
    for name, factor in factors.items():
        out[name] = (out[name] * factor).astype(out[name].dtype)
    return out
```

```python
from contextlib import ExitStack

import numpy as np

import concourse.bass as bass
from concourse import mybir

F32 = mybir.dt.float32
F32R = mybir.dt.float32r
ALU = mybir.AluOpType
ACT = mybir.ActivationFunctionType
IDENT = ACT.Identity

NB, C, L, SD = 64, 64, 1024, 128
NBLK, NLAY, K = 4, 4, 3
NL = NBLK * NLAY
SCALE = 1.0 / float(np.sqrt(C * K ** 2))
EPS = 1e-8
M = L // 2
XW = M + 1
ZPAD = 2
GS = 8
NG = NB // GS
QS = 4
STEPS = [(2 * (p // (2 * NBLK)) + p % 2, (p // 2) % NBLK) for p in range(NG * NBLK)]
NS = len(STEPS)
NN = NS * GS
NQ = NN // QS
NJ = 7
ALLBLUR = [1, 6, 15, 20, 15, 6, 1]
ZP, OP, GPS, VPS = 0, 2, 4, 6


def blur_table():
    t = np.zeros((2 * C, NJ * K), np.float32)
    for half in range(2):
        for j in range(NJ):
            for c in range(K):
                i = 2 * j - 8 - half + 4 + c
                if -6 <= 2 * j - 8 - half <= 2 and 0 <= i < 7:
                    t[half * C:(half + 1) * C, j * K + c] = ALLBLUR[i] / 32.0
    return t


def build(nc, x, style, weights, biases, mod_w, mod_b, ident_d, coef_d, out):
    ctx = ExitStack()
    with ctx:
        def sb(name, shape, dt=F32):
            return ctx.enter_context(nc.sbuf_tensor(name, shape, dt))

        def sem(name):
            return ctx.enter_context(nc.semaphore(name))

        ps = ctx.enter_context(nc.psum_tensor("ps", [128, 8, 512], F32))

        ident = sb("ident", [128, 128])
        coef = sb("coef", [128, NJ * K])
        wT = sb("wT", [128, NL, K, C])
        w1nat = sb("w1nat", [C, NBLK, C * K])
        w0f = sb("w0f", [128, NBLK, 4, C])
        w3f = sb("w3f", [128, NBLK, 2, C])
        w2l = sb("w2l", [128, NBLK, 4, C])
        rh = sb("rh", [128, NBLK, NJ, C], F32R)
        rl = sb("rl", [128, NBLK, NJ, C], F32R)
        names = ["S0", "T1", "bz", "E1", "E2", "D3", "ub", "sbb", "c3", "beta"]
        tab = {n: sb(f"t_{n}", [128, NBLK, NB]) for n in names}
        Bk = sb("Bk", [128, NBLK + 1, NB])
        nBk = sb("nBk", [128, NBLK + 1, NB])

        X = sb("X", [128, 2 * GS, XW])
        raw = [sb(f"raw{i}", [128, 2 * XW]) for i in range(2)]
        ot = [sb(f"ot{i}", [128, L]) for i in range(2)]
        xh = [sb(f"xh{i}", [128, XW + 1], F32R) for i in range(2)]
        xl = [sb(f"xl{i}", [128, XW + 1], F32R) for i in range(2)]
        zh = [sb(f"zh{i}", [128, M + 4], F32R) for i in range(2)]
        zl = [sb(f"zl{i}", [128, M + 4], F32R) for i in range(2)]
        w0q = sb("w0q", [128, QS, 4 * C])
        w0h = [sb(f"w0h{i}", [128, QS, 4 * C], F32R) for i in range(2)]
        w0l = [sb(f"w0l{i}", [128, QS, 4 * C], F32R) for i in range(2)]
        w3q = sb("w3q", [128, 2, QS, C])
        vf = sb("vf", [128, 3, QS, C])
        vh = sb("vh", [128, 3, QS, C], F32R)
        vl = sb("vl", [128, 3, QS, C], F32R)
        gp = sb("gp", [128, QS, 8, C])
        gh = [sb(f"gh{i}", [128, QS, 8, C], F32R) for i in range(2)]
        gl = [sb(f"gl{i}", [128, QS, 8, C], F32R) for i in range(2)]
        xe = sb("xe", [C, GS, 2, 7])
        ze = sb("ze", [C, GS, 2, 7])
        ue = sb("ue", [C, GS, 2, 13])
        b1 = sb("b1", [C, GS, 2, 9])
        b2 = sb("b2", [C, GS, 2, 8])
        ye = sb("ye", [C, GS, 2, 8])
        se = sb("se", [C, GS, 2, 8])
        ve = sb("ve", [C, GS, 2, 5])
        oe = sb("oe", [128, GS, 2, 2])
        en = sb("en", [128, 2, GS, 2])

        def flat(t):
            return t[:, :, :, :].rearrange("p a b c -> p (a b c)")

        def xcols(first, n, width):
            return X[:, first:first + n, :].rearrange("p s m -> p (s m)")[:, 0:width]

        mwn = ot[0][:, :].rearrange("p (l d) -> p l d", l=NL // 2)
        mwT = ot[1][:, :].rearrange("p (l c) -> p l c", l=NL)
        wsq = xcols(0, 6, NL * K * C)[0:C].rearrange("p (l k c) -> p l k c", l=NL, k=K)
        sall = xcols(6, 2, NL * NB).rearrange("p (l b) -> p l b", l=NL)
        wnat = xcols(8, 6, NL * K * C)[0:C].rearrange("p (l w) -> p l w", l=NL)
        dall = xcols(14, 2, NL * NB).rearrange("p (l b) -> p l b", l=NL)
        wsum = wsq[:, :, 0, :]
        var = flat(gp)[:, 0:NL * NB].rearrange("p (l b) -> p l b", l=NL)
        tmp = flat(gp)[:, NL * NB:2 * NL * NB].rearrange("p (l b) -> p l b", l=NL)
        ssq = w0q[0:C, :, :].rearrange("p s c -> p (s c)").rearrange("p (l b) -> p l b", l=NL)
        rf = [t[:, 0:NJ * C].rearrange("p (j c) -> p j c", j=NJ)
              for t in (w0q[:, :, :].rearrange("p s c -> p (s c)"), flat(vf), flat(w3q))]
        small = flat(w3q)
        style_n = small[0:NB, 0:128]
        styleT = small[:, 128:192]
        vecn = small[0:2 * NL, 192:320]
        vec = small[:, 320:352]
        bv = small[0:C, 352:480].rearrange("p (i b) -> p i b", i=2)

        s = {n: sem(f"s_{n}") for n in [
            "c_small", "c_w", "c_mw",
            "p1", "p2", "p3", "p4", "e1", "e2", "e3", "e4", "ts", "sq",
            "bp1", "bp2", "bv1", "bv2", "tabs", "dve_set", "act_set", "rt", "z0",
            "xcopy", "xhi", "xlo", "conv0", "zhi", "zlo", "convg", "xnew",
            "w3q", "w0q", "w0h", "w0l", "V", "vf", "vh", "vl", "G", "gp", "gh", "gl",
            "xe", "zE", "zv", "ze", "uE", "uv", "ye", "sE", "sv", "ve", "oE", "ov", "en", "eap",
            "xb", "oed", "chv", "chp", "cha"]}
        s_raw = [sem(f"s_raw{i}") for i in range(2)]
        s_out = [sem(f"s_out{i}") for i in range(2)]

        def where(n):
            st, i = divmod(n, GS)
            g, k = STEPS[st]
            return st, k, g * GS + i, (g % 2) * GS + i

        def nth(b, k):
            g, i = divmod(b, GS)
            return STEPS.index((g, k)) * GS + i

        def v_at(n):
            return (n + 5) // QS if (n + 5) % QS == 0 and (n + 5) // QS < NQ else None

        def g_at(n):
            return (n + 3) // QS if (n + 3) % QS == 0 and (n + 3) // QS < NQ else None

        def edge_at(n):
            st, i = divmod(n, GS)
            return (st + 1, i - 4) if i >= 4 and st + 1 < NS else (None, None)

        FIRST = -5
        block = ctx.enter_context(nc.Block())

        @block.sync
        def _(sp):
            def load(b):
                r = raw[b % 2]
                if b >= 2:
                    sp.wait_ge(s["xcopy"], b - 1)
                else:
                    sp.wait_ge(s["z0"], 1)
                sp.dma_start(r[0:C, 1:L + 1], x[b]).then_inc(s_raw[b % 2], 16)
                sp.dma_start(r[C:128, 0:L], x[b]).then_inc(s_raw[b % 2], 16)

            def store(j):
                n = nth(2 * j + 1, NBLK - 1)
                sp.wait_ge(s["xnew"], n + 1)
                sp.wait_ge(s["oed"], 2 * j + 2)
                sp.dma_start(out[2 * j:2 * j + 2].rearrange("b c t -> (b c) t"), ot[j % 2][:, :]) \
                    .then_inc(s_out[j % 2], 16)

            sp.dma_start(ident[:, :], ident_d).then_inc(s["c_small"], 16)
            sp.dma_start(coef[:, :], coef_d).then_inc(s["c_small"], 16)
            sp.dma_start(style_n, style).then_inc(s["c_small"], 16)
            for k in range(NBLK):
                for h in range(2):
                    sp.dma_start(vecn[4 * k:4 * k + 4, h * C:(h + 1) * C], mod_b[k]).then_inc(s["c_small"], 16)
                    sp.dma_start(vecn[NL + 4 * k:NL + 4 * k + 4, h * C:(h + 1) * C], biases[k]).then_inc(s["c_small"], 16)
            for b in range(2 * GS):
                load(b)
            for g in range(NG):
                for j in range(g * GS // 2, (g + 1) * GS // 2):
                    store(j)
                if g + 2 < NG:
                    for b in range((g + 2) * GS, (g + 3) * GS):
                        load(b)
            for i in range(2):
                sp.wait_ge(s_out[i], 16 * (NB // 4))

        @block.tensor
        def _(pe):
            pe.wait_ge(s["c_small"], 19 * 16)
            pe.transpose(ps[:, 0, 0:NB], style_n, ident[0:NB, 0:NB])
            pe.transpose(ps[:, 0, 64:64 + 2 * NL], vecn, ident[0:2 * NL, 0:2 * NL]).then_inc(s["p1"], 1)
            pe.wait_ge(s["c_mw"], 16 * NBLK)
            for j in range(NL // 2):
                m = pe.transpose(ps[:, 1 + j // 4, (j % 4) * SD:(j % 4 + 1) * SD], mwn[:, j, :], ident[:, :])
            m.then_inc(s["p1"], 1)
            pe.wait_ge(s["c_w"], 32 * NBLK)
            pe.wait_ge(s["e1"], 2)
            for half in range(2):
                if half:
                    pe.wait_ge(s["e2"], 3)
                for l in range(half * 8, half * 8 + 8):
                    for t in range(K):
                        i = (l % 8) * K + t
                        w = wnat[:, l, :].rearrange("p (i t) -> p i t", t=K)[:, :, t]
                        for h in range(2):
                            m = pe.matmul(ps[h * C:(h + 1) * C, i // 8, (i % 8) * C:(i % 8 + 1) * C], w,
                                          ident[0:C, 0:C], start=True, stop=True, skip_group_check=True)
                m.then_inc(s["p2"], 1)
            for l in range(NL):
                for h in range(2):
                    m = pe.matmul(ps[h * C:(h + 1) * C, 3 + l // 8, (l % 8) * NB:(l % 8 + 1) * NB], mwT[:, l, :],
                                  styleT, start=True, stop=True, skip_group_check=True)
            m.then_inc(s["p3"], 1)
            pe.wait_ge(s["sq"], 2)
            for l in range(NL):
                for h in range(2):
                    m = pe.matmul(ps[h * C:(h + 1) * C, 5 + l // 8, (l % 8) * NB:(l % 8 + 1) * NB], wsum[:, l, :],
                                  ssq[:, l, :], start=True, stop=True, skip_group_check=True)
            m.then_inc(s["p4"], 1)
            for k in range(NBLK):
                pe.wait_ge(s["bv1"], k + 1)
                for t in range(K):
                    m = pe.matmul(ps[0:C, 0, 0:NB], wT[0:C, 4 * k + 2, t, :], bv[:, 0, :],
                                  start=(t == 0), stop=(t == K - 1))
                m.then_inc(s["bp1"], 1)
                pe.wait_ge(s["bv2"], k + 1)
                for h in range(2):
                    for t in range(K):
                        m = pe.matmul(ps[h * C:(h + 1) * C, 1, 0:NB], wT[0:C, 4 * k + 3, t, :], bv[:, 1, :],
                                      start=(t == 0), stop=(t == K - 1), skip_group_check=True)
                m.then_inc(s["bp2"], 1)
            pe.wait_ge(s["tabs"], NBLK)
            pe.wait_ge(s["z0"], 2)

            def products(out_ap, ah, al, bh, bl, first, last):
                pe.matmul(out_ap, ah, bh, start=first, stop=False, skip_group_check=True)
                pe.matmul(out_ap, ah, bl, start=False, stop=False, skip_group_check=True)
                return pe.matmul(out_ap, al, bh, start=False, stop=last, skip_group_check=True)

            def conv0(n):
                q, i, b = n // QS, n % QS, n % 2
                pe.wait_ge(s["xlo"], n + 1)
                if i == 0:
                    pe.wait_ge(s["w0l"], q + 1)
                if n >= 2:
                    pe.wait_ge(s["zlo"], n - 1)
                for d in range(2):
                    w = slice(d * 128, d * 128 + 128)
                    m = products(ps[:, ZP + b, :], w0h[q % 2][:, i, w], w0l[q % 2][:, i, w],
                                 xh[b][:, d:d + M], xl[b][:, d:d + M], d == 0, d == 1)
                m.then_inc(s["conv0"], 1)

            def convg(n):
                q, i, b = n // QS, n % QS, n % 2
                pe.wait_ge(s["zlo"], n + 1)
                if i == 0:
                    pe.wait_ge(s["gl"], q + 1)
                if n >= 2:
                    pe.wait_ge(s["xnew"], n - 1)
                for j, d in enumerate((1, 0, -1, -2)):
                    c = slice(ZPAD + d, ZPAD + d + M)
                    m = products(ps[:, OP + b, :], gh[q % 2][:, i, 2 * j:2 * j + 2, :], gl[q % 2][:, i, 2 * j:2 * j + 2, :],
                                 zh[b][:, c], zl[b][:, c], j == 0, j == 3)
                m.then_inc(s["convg"], 1)

            def v_products(q):
                k = STEPS[q * QS // GS][1]
                pe.wait_ge(s["w3q"], q + 1)
                if q >= 1:
                    pe.wait_ge(s["vf"], q)
                edges_read()
                a = ps[:, VPS, :].rearrange("p (o s c) -> p o s c", o=2, s=QS)
                l0, l2 = w2l[:, k, 0:2, :], w2l[:, k, 2:4, :]
                pe.matmul(a, l0, w3q[:, :, :, :], start=True, stop=False, skip_group_check=True)
                pe.matmul(a[:, 1], l2, w3q[:, 0, :, :], start=False, stop=True, skip_group_check=True)
                pe.matmul(ps[:, VPS + 1, 0:QS * C].rearrange("p (s c) -> p s c", s=QS), l2, w3q[:, 1, :, :],
                          start=True, stop=True, skip_group_check=True).then_inc(s["V"], 1)

            def g_products(q):
                k = STEPS[q * QS // GS][1]
                pe.wait_ge(s["vl"], q + 1)
                if q >= 1:
                    pe.wait_ge(s["gp"], q)
                seen = set()
                for jw in range(NJ - 1):
                    for sg in range(4):
                        for o in range(3):
                            if 4 * sg - 2 * o - 6 != 2 * jw - 8:
                                continue
                            sr = 3 - sg
                            bank, at = GPS + sr // 2, (sr % 2) * QS * C
                            m = products(ps[:, bank, at:at + QS * C],
                                         rh[:, k, jw:jw + 2, :], rl[:, k, jw:jw + 2, :],
                                         vh[:, o, :, :], vl[:, o, :, :],
                                         bank not in seen, False)
                            seen.add(bank)
                m.then_inc(s["G"], 1)

            edges = [0, 0]

            def edges_read():
                if edges[0]:
                    pe.wait_ge(s[("zv", "uv", "sv", "ov")[edges[1]]], edges[0])

            def edge(st, stage):
                k = STEPS[st][1]
                edges_read()
                if v_last[0]:
                    pe.wait_ge(s["vf"], v_last[0])
                base = ps[0:C, VPS + 1, 256:512]
                if stage == 0:
                    pe.wait_ge(s["xe"], st + 1)
                    o = base[:, 0:GS * 10].rearrange("p (s e t) -> p s e t", s=GS, e=2)
                    for t in range(K):
                        m = pe.matmul(o, wT[0:C, 4 * k, t, :], xe[:, :, :, t:t + 5], start=(t == 0), stop=(t == K - 1),
                                      skip_group_check=True)
                    m.then_inc(s["zE"], 1)
                elif stage == 1:
                    pe.wait_ge(s["ze"], st + 1)
                    even = base[:, 0:GS * 12].rearrange("p (s e t) -> p s e t", s=GS, e=2)
                    odd = base[:, GS * 12:GS * 22].rearrange("p (s e t) -> p s e t", s=GS, e=2)
                    w1 = w1nat[:, k, :].rearrange("p (i t) -> p i t", t=K)
                    pe.matmul(even, w1[:, :, 0], ze[:, :, :, 1:7], start=True, stop=False, skip_group_check=True)
                    pe.matmul(even, w1[:, :, 2], ze[:, :, :, 0:6], start=False, stop=True, skip_group_check=True)
                    pe.matmul(odd, w1[:, :, 1], ze[:, :, :, 1:6], start=False, stop=True,
                              skip_group_check=True).then_inc(s["uE"], 1)
                elif stage == 2:
                    pe.wait_ge(s["ye"], st + 1)
                    o = base[:, 0:GS * 12].rearrange("p (s e t) -> p s e t", s=GS, e=2)
                    for t in range(K):
                        m = pe.matmul(o, wT[0:C, 4 * k + 2, t, :], ye[:, :, :, t:t + 6], start=(t == 0),
                                      stop=(t == K - 1), skip_group_check=True)
                    m.then_inc(s["sE"], 1)
                else:
                    pe.wait_ge(s["ve"], st + 1)
                    for h in range(2):
                        o = ps[h * C:(h + 1) * C, VPS + 1, 256:256 + GS * 4].rearrange("p (s e t) -> p s e t", s=GS, e=2)
                        for t in range(K):
                            m = pe.matmul(o, wT[0:C, 4 * k + 3, t, :], ve[:, :, :, t:t + 3:2], start=(t == 0),
                                          stop=(t == K - 1), skip_group_check=True)
                    m.then_inc(s["oE"], 1)
                edges[:] = [st + 1, stage]

            v_last = [0]
            for stage in range(4):
                edge(0, stage)
            for n in range(FIRST, NN):
                if 0 <= n + 1 < NN:
                    conv0(n + 1)
                if v_at(n) is not None:
                    v_products(v_at(n))
                    v_last[0] = v_at(n) + 1
                if g_at(n) is not None:
                    g_products(g_at(n))
                if n >= 0:
                    st, stage = edge_at(n)
                    if st is not None:
                        edge(st, stage)
                    convg(n)

        @block.scalar
        def _(act):
            cha = [0]

            def link(ins):
                cha[0] += 1
                ins.then_inc(s["cha"], 1)
                act.wait_ge(s["cha"], cha[0])

            for k in range(NBLK):
                act.dma_start(mwn[:, 2 * k:2 * k + 2, :], mod_w[k].rearrange("(a l) c d -> (l c) a d", l=2)).then_inc(s["c_mw"], 16)
            for k in range(NBLK):
                act.dma_start(wnat[:, 4 * k:4 * k + 4, :], weights[k].rearrange("l o i t -> o l (i t)")).then_inc(s["c_w"], 16)
                act.dma_start(w1nat[:, k, :], weights[k][1].rearrange("o i t -> o (i t)")).then_inc(s["c_w"], 16)
            wTv = wT[:, :, :, :].rearrange("p l t c -> p (l t c)")
            act.wait_ge(s["p1"], 2)
            mwTv = mwT.rearrange("p l c -> p (l c)")
            act.activation(mwTv[:, 0:512], ps[:, 1, :], ACT.Copy)
            act.activation(mwTv[:, 512:1024], ps[:, 2, :], ACT.Copy).then_inc(s["e1"], 1)
            for half in range(2):
                act.wait_ge(s["p2"], half + 1)
                for j in range(3):
                    a = (half * 3 + j) * 512
                    act.activation(wTv[:, a:a + 512], ps[:, j, :], ACT.Copy).then_inc(s["e2"], 1)
            act.wait_ge(s["chv"], 1)
            act.activation(dall, tmp, ACT.Sqrt).then_inc(s["act_set"], 1)

            act.wait_ge(s["rt"], NBLK)
            act.wait_ge(s["tabs"], NBLK)
            act.wait_ge(s["z0"], 2)

            def xhi(n):
                st, k, b, sl = where(n)
                if k == 0:
                    act.wait_ge(s["xcopy"], b + 1)
                else:
                    act.wait_ge(s["xnew"], n - 2 * GS + 1)
                    act.wait_ge(s["eap"], st - 1)
                if n >= 2:
                    act.wait_ge(s["conv0"], n - 1)
                act.activation(xh[n % 2][:, 0:XW], X[:, sl, :], IDENT, bias=Bk[:, k, b:b + 1]).then_inc(s["xhi"], 1)

            def zhi(n):
                st, k, b, sl = where(n)
                act.wait_ge(s["conv0"], n + 1)
                if n >= 2:
                    act.wait_ge(s["convg"], n - 1)
                act.activation(zh[n % 2][:, ZPAD:ZPAD + M], ps[:, ZP + n % 2, :], IDENT,
                               bias=tab["bz"][:, k, b:b + 1]).then_inc(s["zhi"], 1)

            def w0hi(q):
                act.wait_ge(s["w0q"], q + 1)
                if q >= 2:
                    act.wait_ge(s["conv0"], QS * (q - 1))
                act.activation(w0h[q % 2][:, :, :], w0q[:, :, :], ACT.Copy).then_inc(s["w0h"], 1)

            def vhi(q):
                act.wait_ge(s["vf"], q + 1)
                if q >= 1:
                    act.wait_ge(s["G"], q)
                act.activation(vh[:, :, :, :], vf[:, :, :, :], ACT.Copy).then_inc(s["vh"], 1)

            def ghi(q):
                act.wait_ge(s["gp"], q + 1)
                if q >= 2:
                    act.wait_ge(s["convg"], QS * (q - 1))
                act.activation(gh[q % 2][:, :, :, :], gp[:, :, :, :], ACT.Copy).then_inc(s["gh"], 1)

            xhi(0)
            for n in range(FIRST, NN):
                if v_at(n - 1) is not None:
                    vhi(v_at(n - 1))
                if 0 <= n + 1 < NN:
                    zhi(n + 1)
                if 0 < n + 2 < NN:
                    xhi(n + 2)
                if g_at(n) is not None:
                    w0hi(g_at(n))
                if g_at(n - 1) is not None:
                    ghi(g_at(n - 1))

        @block.vector
        def _(dve):
            chain = [0]

            def link(ins):
                chain[0] += 1
                ins.then_inc(s["dve_set"], 1)
                dve.wait_ge(s["dve_set"], chain[0])

            def bc(a, n):
                return a.unsqueeze(2).broadcast_to([a.shape[0], a.shape[1], n])

            dve.wait_ge(s["p1"], 1)
            dve.tensor_copy(styleT, ps[:, 0, 0:NB])
            dve.tensor_copy(vec, ps[:, 0, 64:64 + 2 * NL]).then_inc(s["e1"], 1)
            dve.wait_ge(s["e2"], 6)
            link(dve.tensor_tensor(wsq, wT[0:C, :, :, :], wT[0:C, :, :, :], ALU.mult))
            link(dve.tensor_tensor(wsum, wsq[:, :, 0, :], wsq[:, :, 1, :], ALU.add))
            dve.tensor_tensor(wsum, wsum, wsq[:, :, 2, :], ALU.add).then_inc(s["sq"], 1)
            dve.wait_ge(s["p3"], 1)
            for h in range(2):
                link(dve.tensor_tensor(sall[:, 8 * h:8 * h + 8, :], ps[:, 3 + h, :].rearrange("p (l b) -> p l b", l=8),
                                       bc(vec[:, 8 * h:8 * h + 8], NB), ALU.add))
            dve.tensor_tensor(ssq, sall[0:C, :, :], sall[0:C, :, :], ALU.mult).then_inc(s["sq"], 1)
            dve.wait_ge(s["p4"], 1)
            link(dve.tensor_scalar(var, ps[:, 5:7, :].rearrange("p k (l b) -> p (k l) b", b=NB), SCALE * SCALE, EPS,
                                   ALU.mult, ALU.add))
            dve.reciprocal(tmp, var).then_inc(s["chv"], 1)
            dve.wait_ge(s["act_set"], 1)
            link(dve.tensor_tensor(tmp, dall, dall, ALU.mult))
            link(dve.tensor_tensor(tmp, tmp, var, ALU.mult))
            link(dve.tensor_scalar(tmp, tmp, -0.5 * SCALE, 1.5 * SCALE, ALU.mult, ALU.add))
            link(dve.tensor_tensor(dall, dall, tmp, ALU.mult))
            link(dve.reciprocal(tmp, dall))

            sv = sall.rearrange("p (k l) b -> p k l b", l=NLAY)
            dv = dall.rearrange("p (k l) b -> p k l b", l=NLAY)
            iv = tmp.rearrange("p (k l) b -> p k l b", l=NLAY)
            bi = vec[:, NL:2 * NL].rearrange("p (k l) -> p k l", l=NLAY)
            T = {n: t[:, :, :] for n, t in tab.items()}
            dve.tensor_copy(T["S0"], sv[:, :, 0, :])
            dve.tensor_tensor(T["T1"], dv[:, :, 0, :], dv[:, :, 1, :], ALU.mult)
            dve.tensor_tensor(T["bz"], iv[:, :, 0, :], bc(bi[:, :, 0], NB), ALU.mult)
            dve.tensor_tensor(T["E1"], sv[:, :, 2, :], sv[:, :, 1, :], ALU.mult)
            dve.tensor_tensor(T["E2"], sv[:, :, 3, :], dv[:, :, 2, :], ALU.mult)
            dve.tensor_copy(T["D3"], dv[:, :, 3, :])
            dve.tensor_tensor(T["ub"], sv[:, :, 2, :], bc(bi[:, :, 1], NB), ALU.mult)
            link(dve.tensor_tensor(T["sbb"], sv[:, :, 3, :], bc(bi[:, :, 2], NB), ALU.mult))
            link(dve.memset(Bk[:, 0, :], 0.0))
            for k in range(NBLK):
                dve.tensor_scalar(bv[:, 0, :], tab["ub"][0:C, k, :], 2.0, None, ALU.mult).then_inc(s["bv1"], 1)
                dve.wait_ge(s["bp1"], k + 1)
                link(dve.tensor_tensor(bv[:, 1, :], ps[0:C, 0, 0:NB], tab["E2"][0:C, k, :], ALU.mult))
                dve.tensor_tensor(bv[:, 1, :], bv[:, 1, :], tab["sbb"][0:C, k, :], ALU.add).then_inc(s["bv2"], 1)
                dve.wait_ge(s["bp2"], k + 1)
                link(dve.tensor_tensor(tab["c3"][:, k, :], ps[:, 1, 0:NB], tab["D3"][:, k, :], ALU.mult))
                link(dve.tensor_scalar(tab["beta"][:, k, :], tab["c3"][:, k, :], vec[:, NL + 4 * k + 3:NL + 4 * k + 4],
                                       None, ALU.add))
                link(dve.tensor_scalar(tab["c3"][:, k, :], tab["c3"][:, k, :], -1.0, None, ALU.mult))
                link(dve.tensor_tensor(Bk[:, k + 1, :], Bk[:, k, :], tab["beta"][:, k, :], ALU.add))
                dve.tensor_scalar(nBk[:, k + 1, :], Bk[:, k + 1, :], -1.0, None, ALU.mult).then_inc(s["tabs"], 1)
            for k in range(NBLK):
                for t in range(K):
                    cf = bc(coef[:, :].rearrange("p (j t) -> p j t", t=K)[:, :, t], C)
                    w = wT[:, 4 * k + 1, t, :].unsqueeze(1).broadcast_to([128, NJ, C])
                    link(dve.tensor_tensor(rf[t], w, cf, ALU.mult))
                link(dve.tensor_tensor(rf[0], rf[0], rf[1], ALU.add))
                link(dve.tensor_tensor(rf[0], rf[0], rf[2], ALU.add))
                link(dve.tensor_copy(rh[:, k, :, :], rf[0]))
                ins = dve.tensor_tensor(rl[:, k, :, :], rf[0], rh[:, k, :, :].bitcast(F32), ALU.subtract)
                link(ins)
            dve.memset(gp[:, :, :, :], 0.0).then_inc(s["rt"], NBLK)
            dve.wait_ge(s["z0"], 2)

            def xlo(n):
                st, k, b, sl = where(n)
                dve.wait_ge(s["xhi"], n + 1)
                dve.scalar_tensor_tensor(xl[n % 2][:, 0:XW], X[:, sl, :], Bk[:, k, b:b + 1],
                                         xh[n % 2][:, 0:XW].bitcast(F32), ALU.add, ALU.subtract).then_inc(s["xlo"], 1)

            def zlo(n):
                st, k, b, sl = where(n)
                dve.wait_ge(s["zhi"], n + 1)
                dve.scalar_tensor_tensor(zl[n % 2][:, ZPAD:ZPAD + M], ps[:, ZP + n % 2, :], tab["bz"][:, k, b:b + 1],
                                         zh[n % 2][:, ZPAD:ZPAD + M].bitcast(F32), ALU.add, ALU.subtract) \
                    .then_inc(s["zlo"], 1)

            def xnew(n):
                st, k, b, sl = where(n)
                dve.wait_ge(s["convg"], n + 1)
                dve.wait_ge(s["en"], st + 1)
                o = ps[:, OP + n % 2, :]
                if k < NBLK - 1:
                    dve.scalar_tensor_tensor(X[:, sl, 1:M], o[:, 1:M], tab["D3"][:, k, b:b + 1], X[:, sl, 1:M],
                                             ALU.mult, ALU.add).then_inc(s["xnew"], 1)
                    return
                dve.wait_ge(s["xb"], b + 1)
                j = b // 2
                if j >= 2:
                    dve.wait_ge(s_out[j % 2], 16 * (j // 2))
                t = ot[j % 2][(b % 2) * C:(b % 2 + 1) * C, :]
                dve.scalar_tensor_tensor(t[:, 3:L - 1:2], o[0:C, 2:M], tab["D3"][0:C, k, b:b + 1], X[0:C, sl, 2:M],
                                         ALU.mult, ALU.add)
                dve.scalar_tensor_tensor(t[:, 2:L - 2:2], o[C:128, 1:M - 1], tab["D3"][C:128, k, b:b + 1],
                                         X[C:128, sl, 1:M - 1], ALU.mult, ALU.add).then_inc(s["xnew"], 1)

            def vfull(q):
                st, k, b, sl = where(q * QS)
                dve.wait_ge(s["V"], q + 1)
                if q >= 1:
                    dve.wait_ge(s["vl"], q)
                e = tab["E1"][:, k, b:b + QS].unsqueeze(1).unsqueeze(3).broadcast_to([128, 3, QS, C])
                pv = ps[:, VPS:VPS + 2, :].rearrange("p k (o s c) -> p (k o) s c", s=QS, c=C)[:, 0:3]
                dve.tensor_tensor(vf[:, :, :, :], pv, e, ALU.mult).then_inc(s["vf"], 1)

            def gplace(q, part):
                st, k, b, sl = where(q * QS)
                if part == 0:
                    dve.wait_ge(s["G"], q + 1)
                    if q >= 1:
                        dve.wait_ge(s["gl"], q)
                pg = ps[:, GPS:GPS + 2, :].rearrange("p k (o s c) -> p s (k o) c", s=QS, c=C)
                for row in ((0, 1), (0, 1))[part]:
                    if part == 0:
                        src, dst = pg[0:C], gp[row * C:row * C + C, :, row:8:2, :]
                        t1, ns = tab["T1"][0:C, k, b:b + QS], 4
                    else:
                        src, dst = pg[C:128, :, 1:4], gp[row * C:row * C + C, :, 1 + row:6 + row:2, :]
                        t1, ns = tab["T1"][C:128, k, b:b + QS], 3
                    t1 = t1.unsqueeze(2).unsqueeze(3).broadcast_to([C, QS, ns, C])
                    ins = dve.tensor_tensor(dst, src, t1, ALU.mult)
                if part == 1:
                    ins.then_inc(s["gp"], 1)

            def edge(st, stage):
                g, k = STEPS[st]
                b = g * GS
                base = ps[0:C, VPS + 1, 256:512]

                def t(name, n):
                    return tab[name][0:C, k, b:b + GS].unsqueeze(2).unsqueeze(3).broadcast_to([C, GS, 2, n])

                if stage == 0:
                    dve.wait_ge(s["zE"], st + 1)
                    dve.tensor_tensor(ze[:, :, :, 1:6], base[:, 0:GS * 10].rearrange("p (s e t) -> p s e t", s=GS, e=2),
                                      t("bz", 5), ALU.add).then_inc(s["zv"], 1)
                elif stage == 1:
                    dve.wait_ge(s["uE"], st + 1)
                    dve.tensor_tensor(ue[:, :, :, 1:12:2], base[:, 0:GS * 12].rearrange("p (s e t) -> p s e t", s=GS, e=2),
                                      t("E1", 6), ALU.mult)
                    dve.tensor_tensor(ue[:, :, :, 2:12:2], base[:, GS * 12:GS * 22].rearrange("p (s e t) -> p s e t", s=GS, e=2),
                                      t("E1", 5), ALU.mult).then_inc(s["uv"], 1)
                elif stage == 2:
                    dve.wait_ge(s["sE"], st + 1)
                    sv_ = base[:, 0:GS * 12].rearrange("p (s e t) -> p s e t", s=GS, e=2)
                    for e in range(2):
                        ins = dve.tensor_tensor(se[:, :, e, 2 - 2 * e:8 - 2 * e], sv_[:, :, e, :],
                                                tab["E2"][0:C, k, b:b + GS].unsqueeze(2).broadcast_to([C, GS, 6]), ALU.mult)
                    ins.then_inc(s["sv"], 1)
                else:
                    dve.wait_ge(s["oE"], st + 1)
                    o = ps[:, VPS + 1, 256:256 + GS * 4].rearrange("p (s t) -> p s t", s=GS)
                    dve.tensor_tensor(oe[:, :, :, :].rearrange("p s e t -> p s (e t)"), o,
                                      tab["D3"][:, k, b:b + GS].unsqueeze(2).broadcast_to([128, GS, 4]), ALU.mult) \
                        .then_inc(s["ov"], 1)

            for stage in range(4):
                edge(0, stage)
            xlo(0)
            for n in range(FIRST, NN):
                if n >= 1:
                    xnew(n - 1)
                if 0 < n + 2 < NN:
                    xlo(n + 2)
                if g_at(n - 1) is not None:
                    gplace(g_at(n - 1), 0)
                if 0 <= n + 1 < NN:
                    zlo(n + 1)
                if g_at(n - 1) is not None:
                    gplace(g_at(n - 1), 1)
                if v_at(n) is not None:
                    vfull(v_at(n))
                if n >= 0:
                    st, stage = edge_at(n)
                    if st is not None:
                        edge(st, stage)
            xnew(NN - 1)

        @block.gpsimd
        def _(pool):
            counts, open_ = {}, {}

            def sig(ins, name="chp", by=1):
                ins.then_inc(s[name], by)
                counts[name] = open_[name] = counts.get(name, 0) + by

            def fence():
                for name, n in open_.items():
                    pool.wait_ge(s[name], n)
                open_.clear()

            def link(ins):
                sig(ins)
                fence()

            for r in raw:
                sig(pool.memset(r[0:C, 0:1], 0.0))
                sig(pool.memset(r[0:C, L + 1:L + 2], 0.0))
                fence()
                link(pool.memset(r[C:128, L:L + 2], 0.0))
            for a in (xe, ze, ue, ye, se):
                link(pool.memset(a[:, :, :, :], 0.0))
            sig(pool.memset(w0f[:, :, :, :], 0.0), "z0")
            sig(pool.memset(w3f[:, :, :, :], 0.0))
            link(pool.memset(w2l[:, :, :, :], 0.0))
            pool.wait_ge(s["c_w"], 32 * NBLK)
            wk = wnat.rearrange("p (k l) (i t) -> p k l t i", l=NLAY, t=K)
            for row, slot, tap in ((0, 0, 0), (0, 1, 1), (1, 1, 0), (0, 2, 2), (1, 2, 1), (1, 3, 2)):
                link(pool.tensor_copy(w2l[row * C:row * C + C, :, slot, :], wk[:, :, 2, tap, :]))
            pool.wait_ge(s["e2"], 6)
            wv = wT[:, :, :, :].rearrange("p (k l) t c -> p k l t c", l=NLAY)
            for row, slot, tap in ((0, 0, 0), (0, 2, 2), (0, 3, 1), (1, 0, 1), (1, 1, 0), (1, 3, 2)):
                h = slice(row * C, row * C + C)
                link(pool.tensor_copy(w0f[h, :, slot, :], wv[h, :, 0, tap, :]))
            for row, slot, tap in ((0, 0, 0), (0, 1, 2), (1, 0, 1)):
                h = slice(row * C, row * C + C)
                link(pool.tensor_copy(w3f[h, :, slot, :], wv[h, :, 3, tap, :]))
            for a in (zh[0], zh[1], zl[0], zl[1]):
                link(pool.memset(a[:, :].bitcast(F32), 0.0))
            sig(pool.memset(en[:, :, :, :], 0.0), "z0")
            pool.wait_ge(s["tabs"], NBLK)
            pool.wait_ge(s["rt"], NBLK)

            def xcopy(b):
                pool.wait_ge(s_raw[b % 2], 32 * (b // 2 + 1))
                if b >= 2 * GS:
                    pool.wait_ge(s["xnew"], nth(b - 2 * GS, NBLK - 1) + 1)
                sl = (b // GS % 2) * GS + b % GS
                sig(pool.tensor_copy(X[:, sl, :], raw[b % 2][:, 0:2 * XW:2]), "xcopy")

            def w3s(q):
                st, k, b, sl = where(q * QS)
                if q >= 1:
                    pool.wait_ge(s["V"], q)
                e = tab["E2"][:, k, b:b + QS].unsqueeze(1).unsqueeze(3).broadcast_to([128, 2, QS, C])
                w = w3f[:, k, :, :].unsqueeze(2).broadcast_to([128, 2, QS, C])
                sig(pool.tensor_tensor(w3q[:, :, :, :], w, e, ALU.mult), "w3q")

            def w0s(q):
                st, k, b, sl = where(q * QS)
                if q >= 1:
                    pool.wait_ge(s["w0l"], q)
                e = tab["S0"][:, k, b:b + QS].unsqueeze(2).broadcast_to([128, QS, 4 * C])
                w = w0f[:, k, :, :].rearrange("p j c -> p (j c)").unsqueeze(1).broadcast_to([128, QS, 4 * C])
                sig(pool.tensor_tensor(w0q[:, :, :], w, e, ALU.mult), "w0q")

            def w0lo(q):
                pool.wait_ge(s["w0h"], q + 1)
                sig(pool.tensor_tensor(w0l[q % 2][:, :, :], w0q[:, :, :], w0h[q % 2][:, :, :].bitcast(F32),
                                   ALU.subtract), "w0l")

            def vlo(q):
                pool.wait_ge(s["vh"], q + 1)
                sig(pool.tensor_tensor(vl[:, :, :, :], vf[:, :, :, :], vh[:, :, :, :].bitcast(F32),
                                   ALU.subtract), "vl")

            def glo(q):
                pool.wait_ge(s["gh"], q + 1)
                sig(pool.tensor_tensor(gl[q % 2][:, :, :, :], gp[:, :, :, :], gh[q % 2][:, :, :, :].bitcast(F32),
                                   ALU.subtract), "gl")

            def x_ends(st):
                g, k = STEPS[st]
                return X[:, (g % 2) * GS:(g % 2 + 1) * GS, :]

            def edge_x(st):
                g, k = STEPS[st]
                b = g * GS
                if k == 0:
                    pool.wait_ge(s["xcopy"], b + GS)
                else:
                    pool.wait_ge(s["xnew"], GS * (st - 1))
                    pool.wait_ge(s["eap"], st - 1)
                if st >= 1:
                    pool.wait_ge(s["zE"], st)
                xv = x_ends(st)
                for e in range(2):
                    lo, hi = (slice(1, 4), slice(0, 3)) if e == 0 else (slice(M - 2, M + 1), slice(M - 3, M))
                    at = 1 - e
                    sig(pool.tensor_tensor(xe[:, :, e, at + 1:at + 6:2], xv[0:C, :, lo],
                                       Bk[0:C, k, b:b + GS].unsqueeze(2).broadcast_to([C, GS, 3]), ALU.add))
                    fence()
                    link(pool.tensor_tensor(xe[:, :, e, at:at + 5:2], xv[C:128, :, hi],
                                            Bk[C:128, k, b:b + GS].unsqueeze(2).broadcast_to([C, GS, 3]), ALU.add))
                xf = xe[:, :, :, :].rearrange("p s e t -> p s (e t)")
                sig(pool.tensor_tensor(xf, xf, tab["S0"][0:C, k, b:b + GS].unsqueeze(2).broadcast_to([C, GS, 14]),
                                   ALU.mult), "xe")

            def edge_z(st):
                g, k = STEPS[st]
                b = g * GS
                pool.wait_ge(s["zv"], st + 1)
                zf = ze[:, :, :, :].rearrange("p s e t -> p s (e t)")
                sig(pool.tensor_tensor(zf, zf, tab["T1"][0:C, k, b:b + GS].unsqueeze(2).broadcast_to([C, GS, 14]),
                                   ALU.mult), "ze")

            def blur(dst, src, n, off, last, factor, name):
                a1, a2 = b1[:, :, :, 0:n + 2], b2[:, :, :, 0:n + 1]
                for e in range(2):
                    o = off[e]
                    ins = pool.tensor_tensor(a1[:, :, e, :], src[:, :, e, o:o + n + 2], src[:, :, e, o + 1:o + n + 3], ALU.add)
                    sig(ins)
                fence()
                link(pool.tensor_tensor(a2, b1[:, :, :, 0:n + 1], b1[:, :, :, 1:n + 2], ALU.add))
                link(pool.tensor_scalar(a2, a2, factor, None, ALU.mult))
                for e in range(2):
                    o = last[e]
                    ins = pool.tensor_tensor(dst[:, :, e, o:o + n], b2[:, :, e, 0:n], b2[:, :, e, 1:n + 1], ALU.add)
                    sig(ins, name if e else "chp")

            def edge_u(st):
                g, k = STEPS[st]
                b = g * GS
                pool.wait_ge(s["uv"], st + 1)
                uv = ue[:, :, :, 1:12]
                link(pool.tensor_tensor(uv, uv, tab["ub"][0:C, k, b:b + GS].unsqueeze(2).unsqueeze(3)
                                        .broadcast_to([C, GS, 2, 11]), ALU.add))
                blur(ye, ue, 7, (0, 3), (1, 0), 0.25, "ye")

            def edge_s(st):
                g, k = STEPS[st]
                b = g * GS
                pool.wait_ge(s["sv"], st + 1)
                for e in range(2):
                    sv_ = se[:, :, e, 2 - 2 * e:8 - 2 * e]
                    ins = pool.tensor_tensor(sv_, sv_, tab["sbb"][0:C, k, b:b + GS].unsqueeze(2).broadcast_to([C, GS, 6]), ALU.add)
                    sig(ins)
                fence()
                blur(ve, se, 5, (0, 0), (0, 0), 0.125, "ve")

            def edge_o(st):
                g, k = STEPS[st]
                b = g * GS
                xv = x_ends(st)
                pool.wait_ge(s["ov"], st + 1)
                of = oe[:, :, :, :].rearrange("p s e t -> p s (e t)")
                link(pool.tensor_tensor(of, of, tab["c3"][:, k, b:b + GS].unsqueeze(2).broadcast_to([128, GS, 4]), ALU.add))
                ev = en[:, st % 2, :, :]
                sig(pool.tensor_tensor(ev[0:C], oe[0:C, :, :, 1], xv[0:C, :, 1:M + 1:M - 1], ALU.add))
                fence()
                ins = pool.tensor_tensor(ev[C:128], oe[C:128, :, :, 0], xv[C:128, :, 0:M:M - 1], ALU.add)
                if k == NBLK - 1:
                    link(ins)
                    ins = pool.tensor_tensor(ev, ev, Bk[:, NBLK, b:b + GS].unsqueeze(2).broadcast_to([128, GS, 2]), ALU.add)
                sig(ins, "en")
                fence()

            def edge_apply(st):
                g, k = STEPS[st]
                b = g * GS
                pool.wait_ge(s["xnew"], GS * (st + 1))
                xv, ev = x_ends(st), en[:, st % 2, :, :]
                fence()
                if k < NBLK - 1:
                    link(pool.tensor_copy(xv[C:128, :, 0:M:M - 1], ev[C:128]))
                    link(pool.tensor_copy(xv[C:128, :, M], nBk[C:128, k + 1, b:b + GS]))
                    sig(pool.tensor_copy(xv[0:C, :, 1:M + 1:M - 1], ev[0:C]))
                    sig(pool.tensor_copy(xv[0:C, :, 0], nBk[0:C, k + 1, b:b + GS]), "eap")
                else:
                    sig(pool.memset(b1[:, 0, 0, 0:1], 0.0), "eap")
                fence()

            def finish(n):
                st, k, b, sl = where(n)
                pool.wait_ge(s["xlo"], n + 1)
                pool.wait_ge(s["en"], st + 1)
                sig(pool.tensor_scalar(X[:, sl, :], X[:, sl, :], Bk[:, NBLK, b:b + 1], None, ALU.add), "xb")
                j = b // 2
                if j >= 2:
                    pool.wait_ge(s_out[j % 2], 16 * (j // 2))
                t = ot[j % 2][(b % 2) * C:(b % 2 + 1) * C, :]
                ev = en[:, st % 2, b % GS, :]
                fence()
                link(pool.tensor_copy(t[:, 0:L - 1:L - 2], ev[C:128]))
                sig(pool.tensor_copy(t[:, 1:L:L - 2], ev[0:C]), "oed")
                fence()

            for b in range(2 * GS):
                xcopy(b)
                if b == GS - 1:
                    edge_x(0)
                    edge_z(0)
                    edge_u(0)
                    edge_s(0)
                    edge_o(0)
            w3s(0)
            for n in range(FIRST, NN):
                st, i = divmod(n, GS)
                if n >= 0:
                    if STEPS[st][1] == NBLK - 1:
                        finish(n)
                    if st >= 1 and STEPS[st - 1][1] == NBLK - 1 and STEPS[st - 1][0] + 2 < NG and i < 4:
                        for b in range(2):
                            xcopy((STEPS[st - 1][0] + 2) * GS + 2 * i + b)
                if v_at(n - 1) is not None:
                    vlo(v_at(n - 1))
                if g_at(n) is not None:
                    w0s(g_at(n))
                    w0lo(g_at(n))
                if g_at(n - 1) is not None:
                    glo(g_at(n - 1))
                if v_at(n + 2) is not None and v_at(n + 2) > 0:
                    w3s(v_at(n + 2))
                if n >= 1 and n % GS == 1 and st >= 1:
                    edge_apply(st - 1)
                if n >= 0 and st + 1 < NS:
                    if i == 3:
                        edge_x(st + 1)
                    if i == 4:
                        edge_z(st + 1)
                    if i == 5:
                        edge_u(st + 1)
                    if i == 6:
                        edge_s(st + 1)
                    if i == 7:
                        edge_o(st + 1)


def kernel(**inputs):
    import concourse.bacc as bacc
    from concourse.bass_utils import run_bass_kernel_spmd

    nc = bacc.Bacc("TRN2", target_bir_lowering=False, num_devices=1)
    arrays = {}

    def dram(name, a):
        a = np.ascontiguousarray(a)
        arrays[name] = a
        return nc.dram_tensor(name, a.shape, mybir.dt.from_np(a.dtype), kind="ExternalInput").ap()

    x = dram("x_in", inputs["x"])
    style = dram("style_in", inputs["cond_512"])
    weights, biases, mod_w, mod_b = (
        [dram(f"{what}{k}_in", inputs[f"L{k}_cond_{what}"]) for k in range(NBLK)]
        for what in ("weights", "biases", "mod_w", "mod_b"))
    ident_d = dram("ident_in", np.eye(128, dtype=np.float32))
    coef_d = dram("coef_in", blur_table())
    out = nc.dram_tensor("out_x", (NB, C, L), F32, kind="ExternalOutput").ap()
    build(nc, x, style, weights, biases, mod_w, mod_b, ident_d, coef_d, out)
    r = run_bass_kernel_spmd(nc, [arrays], core_ids=[0])
    return r.results[0]["out_x"]
```

```python
from contextlib import ExitStack

import numpy as np

import concourse.bass as bass
from concourse import mybir

F32 = mybir.dt.float32
F32R = mybir.dt.float32r
ALU = mybir.AluOpType
ACT = mybir.ActivationFunctionType
IDENT = ACT.Identity

NB, C, L, SD = 64, 64, 1024, 128
NBLK, NLAY, K = 4, 4, 3
NL = NBLK * NLAY
SCALE = 1.0 / float(np.sqrt(C * K ** 2))
EPS = 1e-8
M = L // 2
XW = M + 1
ZPAD = 2
GS = 8
NG = NB // GS
NR = 3
QS = 4
STEPS = [(2 * (p // (2 * NBLK)) + p % 2, (p // 2) % NBLK) for p in range(NG * NBLK)]
NS = len(STEPS)
NN = NS * GS
NQ = NN // QS
V_LEAD, G_LEAD = 6, 4
EDGE_SLOTS = (3, 4, 6, 7)
NJ = 7
ALLBLUR = [1, 6, 15, 20, 15, 6, 1]
ZP, OP, VG, EP = 0, 2, 4, 6


def blur_table():
    t = np.zeros((2 * C, NJ * K), np.float32)
    for half in range(2):
        for j in range(NJ):
            for c in range(K):
                i = 2 * j - 8 - half + 4 + c
                if -6 <= 2 * j - 8 - half <= 2 and 0 <= i < 7:
                    t[half * C:(half + 1) * C, j * K + c] = ALLBLUR[i] / 32.0
    return t


def build(nc, x, style, weights, biases, mod_w, mod_b, ident_d, coef_d, out):
    ctx = ExitStack()
    with ctx:
        def sb(name, shape, dt=F32):
            return ctx.enter_context(nc.sbuf_tensor(name, shape, dt))

        def sem(name):
            return ctx.enter_context(nc.semaphore(name))

        ps = ctx.enter_context(nc.psum_tensor("ps", [128, 8, 512], F32))

        coef = sb("coef", [128, NJ * K])
        wT = sb("wT", [128, NL, K, C])
        w1nat = sb("w1nat", [C, NBLK, C * K])
        w0f = sb("w0f", [128, NBLK, 4, C])
        w3f = sb("w3f", [128, NBLK, 2, C])
        w2l = sb("w2l", [128, NBLK, 4, C])
        rh = sb("rh", [128, NBLK, NJ, C], F32R)
        rl = sb("rl", [128, NBLK, NJ, C], F32R)
        names = ["S0", "T1", "bz", "E1", "E2", "D3", "ub", "sbb", "c3"]
        tab = {n: sb(f"t_{n}", [128, NBLK, NB]) for n in names}
        Bk = sb("Bk", [128, NBLK + 1, NB])
        nBk = sb("nBk", [128, NBLK + 1, NB])

        X = sb("X", [128, NR * GS, XW])
        raw = [sb(f"raw{i}", [128, 2 * XW]) for i in range(2)]
        ot = [sb(f"ot{i}", [128, L]) for i in range(2)]
        xh = [sb(f"xh{i}", [128, XW + 1], F32R) for i in range(2)]
        xl = [sb(f"xl{i}", [128, XW + 1], F32R) for i in range(2)]
        zh = [sb(f"zh{i}", [128, M + 4], F32R) for i in range(2)]
        zl = [sb(f"zl{i}", [128, M + 4], F32R) for i in range(2)]
        w0q = sb("w0q", [128, QS, 4 * C])
        w0h = [sb(f"w0h{i}", [128, QS, 4 * C], F32R) for i in range(2)]
        w0l = [sb(f"w0l{i}", [128, QS, 4 * C], F32R) for i in range(2)]
        w3q = sb("w3q", [128, 2, QS, C])
        vf = sb("vf", [128, 3, QS, C])
        vh = sb("vh", [128, 3, QS, C], F32R)
        vl = sb("vl", [128, 3, QS, C], F32R)
        gp = sb("gp", [128, QS, 8, C])
        gh = [sb(f"gh{i}", [128, QS, 8, C], F32R) for i in range(2)]
        gl = [sb(f"gl{i}", [128, QS, 8, C], F32R) for i in range(2)]
        xe = sb("xe", [C, GS, 2, 7])
        ze = sb("ze", [C, GS, 2, 7])
        ue = sb("ue", [C, GS, 2, 13])
        b1 = sb("b1", [C, GS, 2, 9])
        b2 = sb("b2", [C, GS, 2, 8])
        ye = sb("ye", [C, GS, 2, 8])
        se = sb("se", [C, GS, 2, 8])
        ve = sb("ve", [C, GS, 2, 5])
        oe = sb("oe", [128, GS, 2, 2])
        en = sb("en", [128, 2, GS, 2])

        def flat(t):
            return t[:, :, :, :].rearrange("p a b c -> p (a b c)")

        def xcols(first, n, width):
            return X[:, first:first + n, :].rearrange("p s m -> p (s m)")[:, 0:width]

        mwn = ot[0][:, :].rearrange("p (l d) -> p l d", l=NL // 2)
        mwT = ot[1][:, :].rearrange("p (l c) -> p l c", l=NL)
        wsq = xcols(8, 6, NL * K * C)[0:C].rearrange("p (l k c) -> p l k c", l=NL, k=K)
        sall = xcols(14, 2, NL * NB).rearrange("p (l b) -> p l b", l=NL)
        wnat = xcols(16, 6, NL * K * C)[0:C].rearrange("p (l w) -> p l w", l=NL)
        dall = xcols(22, 2, NL * NB).rearrange("p (l b) -> p l b", l=NL)
        ident = flat(vf)[:, 0:128]
        beta = flat(vf)[:, 128:128 + NB]
        wsum = wsq[:, :, 0, :]
        var = flat(gp)[:, 0:NL * NB].rearrange("p (l b) -> p l b", l=NL)
        tmp = flat(gp)[:, NL * NB:2 * NL * NB].rearrange("p (l b) -> p l b", l=NL)
        ssq = w0q[0:C, :, :].rearrange("p s c -> p (s c)").rearrange("p (l b) -> p l b", l=NL)
        rf = [t[:, 0:NJ * C].rearrange("p (j c) -> p j c", j=NJ)
              for t in (w0q[:, :, :].rearrange("p s c -> p (s c)"), flat(vf), flat(w3q))]
        small = flat(w3q)
        style_n = small[0:NB, 0:128]
        styleT = small[:, 128:192]
        vecn = small[0:2 * NL, 192:320]
        vec = small[:, 320:352]
        bv = small[0:C, 352:480].rearrange("p (i b) -> p i b", i=2)

        s = {n: sem(f"s_{n}") for n in [
            "c_small", "c_w", "c_mw",
            "p1", "p2", "p3", "p4", "e1", "e2", "e3", "e4", "ts", "sq",
            "bp1", "bp2", "bv1", "bv2", "tabs", "dve_set", "act_set", "rt", "z0",
            "xcopy", "xhi", "xlo", "conv0", "zhi", "zlo", "convg", "xnew",
            "w3q", "w0q", "w0h", "w0l", "V", "vf", "vh", "vl", "G", "gp", "gh", "gl",
            "xe", "zE", "zv", "ze", "uE", "uv", "ye", "sE", "sv", "ve", "oE", "ov", "en", "eap",
            "xb", "oed", "chv", "chp", "cha"]}
        s_raw = [sem(f"s_raw{i}") for i in range(2)]
        s_out = [sem(f"s_out{i}") for i in range(2)]

        def where(n):
            st, i = divmod(n, GS)
            g, k = STEPS[st]
            return st, k, g * GS + i, (g % NR) * GS + i

        def nth(b, k):
            g, i = divmod(b, GS)
            return STEPS.index((g, k)) * GS + i

        def loads_at(n):
            st, i = divmod(n, GS)
            if st + 2 < NS and STEPS[st + 2][1] == 0 and STEPS[st + 2][0] >= 2:
                return STEPS[st + 2][0] * GS + i
            return None

        def v_at(n):
            q, i = divmod(n + V_LEAD, QS)
            return q if i == 0 and 0 <= q < NQ else None

        def g_at(n):
            q, i = divmod(n + G_LEAD, QS)
            return q if i == 0 and 0 <= q < NQ else None

        def edge_at(n):
            st, i = divmod(n, GS)
            return (st + 1, EDGE_SLOTS.index(i)) if n >= 0 and i in EDGE_SLOTS and st + 1 < NS else (None, None)

        FIRST = -V_LEAD
        block = ctx.enter_context(nc.Block())

        @block.sync
        def _(sp):
            def load(b):
                r = raw[b % 2]
                if b >= 2:
                    sp.wait_ge(s["xcopy"], b - 1)
                else:
                    sp.wait_ge(s["z0"], 1)
                sp.dma_start(r[0:C, 1:L + 1], x[b]).then_inc(s_raw[b % 2], 16)
                sp.dma_start(r[C:128, 0:L], x[b]).then_inc(s_raw[b % 2], 16)

            def store(j):
                n = nth(2 * j + 1, NBLK - 1)
                sp.wait_ge(s["xnew"], n + 1)
                sp.wait_ge(s["oed"], 2 * j + 2)
                sp.dma_start(out[2 * j:2 * j + 2].rearrange("b c t -> (b c) t"), ot[j % 2][:, :]) \
                    .then_inc(s_out[j % 2], 16)

            sp.dma_start(ident[:, :], ident_d).then_inc(s["c_small"], 16)
            sp.dma_start(coef[:, :], coef_d).then_inc(s["c_small"], 16)
            sp.dma_start(style_n, style).then_inc(s["c_small"], 16)
            for k in range(NBLK):
                for h in range(2):
                    sp.dma_start(vecn[4 * k:4 * k + 4, h * C:(h + 1) * C], mod_b[k]).then_inc(s["c_small"], 16)
                    sp.dma_start(vecn[NL + 4 * k:NL + 4 * k + 4, h * C:(h + 1) * C], biases[k]).then_inc(s["c_small"], 16)
            for b in range(2 * GS):
                load(b)
            for n in range(NN + 1):
                if n < NN and loads_at(n) is not None:
                    load(loads_at(n))
                if n >= 1 and n % 2 == 0 and where(n - 1)[1] == NBLK - 1:
                    store(where(n - 1)[2] // 2)
            for i in range(2):
                sp.wait_ge(s_out[i], 16 * (NB // 4))

        @block.tensor
        def _(pe):
            pe.wait_ge(s["c_small"], 19 * 16)
            pe.transpose(ps[:, 0, 0:NB], style_n, ident[0:NB, 0:NB])
            pe.transpose(ps[:, 0, 64:64 + 2 * NL], vecn, ident[0:2 * NL, 0:2 * NL]).then_inc(s["p1"], 1)
            pe.wait_ge(s["c_mw"], 16 * NBLK)
            for j in range(NL // 2):
                m = pe.transpose(ps[:, 1 + j // 4, (j % 4) * SD:(j % 4 + 1) * SD], mwn[:, j, :], ident[:, :])
            m.then_inc(s["p1"], 1)
            pe.wait_ge(s["c_w"], 32 * NBLK)
            pe.wait_ge(s["e1"], 2)
            for half in range(2):
                if half:
                    pe.wait_ge(s["e2"], 3)
                for l in range(half * 8, half * 8 + 8):
                    for t in range(K):
                        i = (l % 8) * K + t
                        w = wnat[:, l, :].rearrange("p (i t) -> p i t", t=K)[:, :, t]
                        for h in range(2):
                            m = pe.matmul(ps[h * C:(h + 1) * C, i // 8, (i % 8) * C:(i % 8 + 1) * C], w,
                                          ident[0:C, 0:C], start=True, stop=True, skip_group_check=True)
                m.then_inc(s["p2"], 1)
            for l in range(NL):
                for h in range(2):
                    m = pe.matmul(ps[h * C:(h + 1) * C, 3 + l // 8, (l % 8) * NB:(l % 8 + 1) * NB], mwT[:, l, :],
                                  styleT, start=True, stop=True, skip_group_check=True)
            m.then_inc(s["p3"], 1)
            pe.wait_ge(s["sq"], 2)
            for l in range(NL):
                for h in range(2):
                    m = pe.matmul(ps[h * C:(h + 1) * C, 5 + l // 8, (l % 8) * NB:(l % 8 + 1) * NB], wsum[:, l, :],
                                  ssq[:, l, :], start=True, stop=True, skip_group_check=True)
            m.then_inc(s["p4"], 1)
            for k in range(NBLK):
                pe.wait_ge(s["bv1"], k + 1)
                for t in range(K):
                    m = pe.matmul(ps[0:C, 0, 0:NB], wT[0:C, 4 * k + 2, t, :], bv[:, 0, :],
                                  start=(t == 0), stop=(t == K - 1))
                m.then_inc(s["bp1"], 1)
                pe.wait_ge(s["bv2"], k + 1)
                for h in range(2):
                    for t in range(K):
                        m = pe.matmul(ps[h * C:(h + 1) * C, 1, 0:NB], wT[0:C, 4 * k + 3, t, :], bv[:, 1, :],
                                      start=(t == 0), stop=(t == K - 1), skip_group_check=True)
                m.then_inc(s["bp2"], 1)
            pe.wait_ge(s["tabs"], NBLK)
            pe.wait_ge(s["z0"], 2)

            def products(out_ap, ah, al, bh, bl, first, last):
                pe.matmul(out_ap, ah, bh, start=first, stop=False, skip_group_check=True)
                pe.matmul(out_ap, ah, bl, start=False, stop=False, skip_group_check=True)
                return pe.matmul(out_ap, al, bh, start=False, stop=last, skip_group_check=True)

            def conv0(n):
                q, i, b = n // QS, n % QS, n % 2
                pe.wait_ge(s["xlo"], n + 1)
                if i == 0:
                    pe.wait_ge(s["w0l"], q + 1)
                if n >= 2:
                    pe.wait_ge(s["zlo"], n - 1)
                for d in range(2):
                    w = slice(d * 128, d * 128 + 128)
                    m = products(ps[:, ZP + b, :], w0h[q % 2][:, i, w], w0l[q % 2][:, i, w],
                                 xh[b][:, d:d + M], xl[b][:, d:d + M], d == 0, d == 1)
                m.then_inc(s["conv0"], 1)

            def convg(n):
                q, i, b = n // QS, n % QS, n % 2
                pe.wait_ge(s["zlo"], n + 1)
                if i % 2 == 0:
                    pe.wait_ge(s["gl"], 2 * q + 1 + i // 2)
                if n >= 2:
                    pe.wait_ge(s["xnew"], n - 1)
                for j, d in enumerate((1, 0, -1, -2)):
                    c = slice(ZPAD + d, ZPAD + d + M)
                    m = products(ps[:, OP + b, :], gh[q % 2][:, i, 2 * j:2 * j + 2, :], gl[q % 2][:, i, 2 * j:2 * j + 2, :],
                                 zh[b][:, c], zl[b][:, c], j == 0, j == 3)
                m.then_inc(s["convg"], 1)

            def v_products(q):
                k = STEPS[q * QS // GS][1]
                pe.wait_ge(s["w3q"], q + 1)
                if q >= 1:
                    pe.wait_ge(s["gp"], q)
                a = ps[:, VG, :].rearrange("p (o s c) -> p o s c", o=2, s=QS)
                l0, l2 = w2l[:, k, 0:2, :], w2l[:, k, 2:4, :]
                pe.matmul(a, l0, w3q[:, :, :, :], start=True, stop=False, skip_group_check=True)
                pe.matmul(a[:, 1], l2, w3q[:, 0, :, :], start=False, stop=True, skip_group_check=True)
                pe.matmul(ps[:, VG + 1, 0:QS * C].rearrange("p (s c) -> p s c", s=QS), l2, w3q[:, 1, :, :],
                          start=True, stop=True, skip_group_check=True).then_inc(s["V"], 1)

            def g_products(q):
                k = STEPS[q * QS // GS][1]
                pe.wait_ge(s["vl"], q + 1)
                seen = set()
                for jw in range(NJ - 1):
                    for sg in range(4):
                        for o in range(3):
                            if 4 * sg - 2 * o - 6 != 2 * jw - 8:
                                continue
                            sr = 3 - sg
                            bank, at = VG + sr // 2, (sr % 2) * QS * C
                            m = products(ps[:, bank, at:at + QS * C],
                                         rh[:, k, jw:jw + 2, :], rl[:, k, jw:jw + 2, :],
                                         vh[:, o, :, :], vl[:, o, :, :],
                                         bank not in seen, False)
                            seen.add(bank)
                m.then_inc(s["G"], 1)

            def edge(st, stage):
                k = STEPS[st][1]
                bank = EP + stage % 2
                base = ps[0:C, bank, :]
                if stage == 0:
                    pe.wait_ge(s["xe"], st + 1)
                    o = base[:, 0:GS * 10].rearrange("p (s e t) -> p s e t", s=GS, e=2)
                    for t in range(K):
                        m = pe.matmul(o, wT[0:C, 4 * k, t, :], xe[:, :, :, t:t + 5], start=(t == 0), stop=(t == K - 1),
                                      skip_group_check=True)
                    m.then_inc(s["zE"], 1)
                elif stage == 1:
                    pe.wait_ge(s["ze"], st + 1)
                    even = base[:, 0:GS * 12].rearrange("p (s e t) -> p s e t", s=GS, e=2)
                    odd = base[:, GS * 12:GS * 22].rearrange("p (s e t) -> p s e t", s=GS, e=2)
                    w1 = w1nat[:, k, :].rearrange("p (i t) -> p i t", t=K)
                    pe.matmul(even, w1[:, :, 0], ze[:, :, :, 1:7], start=True, stop=False, skip_group_check=True)
                    pe.matmul(even, w1[:, :, 2], ze[:, :, :, 0:6], start=False, stop=True, skip_group_check=True)
                    pe.matmul(odd, w1[:, :, 1], ze[:, :, :, 1:6], start=False, stop=True,
                              skip_group_check=True).then_inc(s["uE"], 1)
                elif stage == 2:
                    pe.wait_ge(s["ye"], st + 1)
                    o = base[:, 0:GS * 12].rearrange("p (s e t) -> p s e t", s=GS, e=2)
                    for t in range(K):
                        m = pe.matmul(o, wT[0:C, 4 * k + 2, t, :], ye[:, :, :, t:t + 6], start=(t == 0),
                                      stop=(t == K - 1), skip_group_check=True)
                    m.then_inc(s["sE"], 1)
                else:
                    pe.wait_ge(s["ve"], st + 1)
                    for h in range(2):
                        o = ps[h * C:(h + 1) * C, bank, 0:GS * 4].rearrange("p (s e t) -> p s e t", s=GS, e=2)
                        for t in range(K):
                            m = pe.matmul(o, wT[0:C, 4 * k + 3, t, :], ve[:, :, :, t:t + 3:2], start=(t == 0),
                                          stop=(t == K - 1), skip_group_check=True)
                    m.then_inc(s["oE"], 1)

            for stage in range(4):
                edge(0, stage)
            for n in range(FIRST, NN):
                if 0 <= n + 1 < NN:
                    conv0(n + 1)
                if v_at(n) is not None:
                    v_products(v_at(n))
                if g_at(n) is not None:
                    g_products(g_at(n))
                if n >= 0:
                    st, stage = edge_at(n)
                    if st is not None:
                        edge(st, stage)
                    convg(n)

        @block.scalar
        def _(act):
            cha = [0]

            def link(ins):
                cha[0] += 1
                ins.then_inc(s["cha"], 1)
                act.wait_ge(s["cha"], cha[0])

            for k in range(NBLK):
                act.dma_start(mwn[:, 2 * k:2 * k + 2, :], mod_w[k].rearrange("(a l) c d -> (l c) a d", l=2)).then_inc(s["c_mw"], 16)
            for k in range(NBLK):
                act.dma_start(wnat[:, 4 * k:4 * k + 4, :], weights[k].rearrange("l o i t -> o l (i t)")).then_inc(s["c_w"], 16)
                act.dma_start(w1nat[:, k, :], weights[k][1].rearrange("o i t -> o (i t)")).then_inc(s["c_w"], 16)
            wTv = wT[:, :, :, :].rearrange("p l t c -> p (l t c)")
            act.wait_ge(s["p1"], 2)
            mwTv = mwT.rearrange("p l c -> p (l c)")
            act.activation(mwTv[:, 0:512], ps[:, 1, :], ACT.Copy)
            act.activation(mwTv[:, 512:1024], ps[:, 2, :], ACT.Copy).then_inc(s["e1"], 1)
            for half in range(2):
                act.wait_ge(s["p2"], half + 1)
                for j in range(3):
                    a = (half * 3 + j) * 512
                    act.activation(wTv[:, a:a + 512], ps[:, j, :], ACT.Copy).then_inc(s["e2"], 1)
            act.wait_ge(s["chv"], 1)
            act.activation(dall, tmp, ACT.Sqrt).then_inc(s["act_set"], 1)

            act.wait_ge(s["rt"], NBLK)
            act.wait_ge(s["tabs"], NBLK)
            act.wait_ge(s["z0"], 2)

            def xhi(n):
                st, k, b, sl = where(n)
                if k == 0:
                    act.wait_ge(s["xcopy"], b + 1)
                else:
                    act.wait_ge(s["xnew"], n - 2 * GS + 1)
                    act.wait_ge(s["eap"], st - 1)
                if n >= 2:
                    act.wait_ge(s["conv0"], n - 1)
                act.activation(xh[n % 2][:, 0:XW], X[:, sl, :], IDENT, bias=Bk[:, k, b:b + 1]).then_inc(s["xhi"], 1)

            def zhi(n):
                st, k, b, sl = where(n)
                act.wait_ge(s["conv0"], n + 1)
                if n >= 2:
                    act.wait_ge(s["convg"], n - 1)
                act.activation(zh[n % 2][:, ZPAD:ZPAD + M], ps[:, ZP + n % 2, :], IDENT,
                               bias=tab["bz"][:, k, b:b + 1]).then_inc(s["zhi"], 1)

            def w0hi(q):
                st, k, b, sl = where(q * QS)
                if q >= 1:
                    act.wait_ge(s["w0l"], q)
                for i in range(QS):
                    ins = act.activation(w0q[:, i, :], w0f[:, k, :, :].rearrange("p j c -> p (j c)"), ACT.Copy,
                                         scale=tab["S0"][:, k, b + i:b + i + 1])
                ins.then_inc(s["w0q"], 1)
                act.wait_ge(s["w0q"], q + 1)
                if q >= 2:
                    act.wait_ge(s["conv0"], QS * (q - 1))
                act.activation(w0h[q % 2][:, :, :], w0q[:, :, :], ACT.Copy).then_inc(s["w0h"], 1)

            def vhi(q):
                act.wait_ge(s["vf"], q + 1)
                if q >= 1:
                    act.wait_ge(s["G"], q)
                act.activation(vh[:, :, :, :], vf[:, :, :, :], ACT.Copy).then_inc(s["vh"], 1)

            def ghi(q):
                act.wait_ge(s["gp"], q + 1)
                if q >= 2:
                    act.wait_ge(s["convg"], QS * (q - 1))
                for h in (slice(0, 2), slice(2, 4)):
                    act.activation(gh[q % 2][:, h, :, :], gp[:, h, :, :], ACT.Copy).then_inc(s["gh"], 1)

            xhi(0)
            for n in range(FIRST, NN):
                if g_at(n - 2) is not None:
                    ghi(g_at(n - 2))
                if 0 <= n + 1 < NN:
                    zhi(n + 1)
                if 0 < n + 2 < NN:
                    xhi(n + 2)
                if v_at(n - 1) is not None:
                    vhi(v_at(n - 1))
                if g_at(n) is not None:
                    w0hi(g_at(n))

        @block.vector
        def _(dve):
            chain = [0]

            def link(ins):
                chain[0] += 1
                ins.then_inc(s["dve_set"], 1)
                dve.wait_ge(s["dve_set"], chain[0])

            def bc(a, n):
                return a.unsqueeze(2).broadcast_to([a.shape[0], a.shape[1], n])

            dve.wait_ge(s["p1"], 1)
            dve.tensor_copy(styleT, ps[:, 0, 0:NB])
            dve.tensor_copy(vec, ps[:, 0, 64:64 + 2 * NL]).then_inc(s["e1"], 1)
            dve.wait_ge(s["e2"], 6)
            link(dve.tensor_tensor(wsq, wT[0:C, :, :, :], wT[0:C, :, :, :], ALU.mult))
            link(dve.tensor_tensor(wsum, wsq[:, :, 0, :], wsq[:, :, 1, :], ALU.add))
            dve.tensor_tensor(wsum, wsum, wsq[:, :, 2, :], ALU.add).then_inc(s["sq"], 1)
            dve.wait_ge(s["p3"], 1)
            for h in range(2):
                link(dve.tensor_tensor(sall[:, 8 * h:8 * h + 8, :], ps[:, 3 + h, :].rearrange("p (l b) -> p l b", l=8),
                                       bc(vec[:, 8 * h:8 * h + 8], NB), ALU.add))
            dve.tensor_tensor(ssq, sall[0:C, :, :], sall[0:C, :, :], ALU.mult).then_inc(s["sq"], 1)
            dve.wait_ge(s["p4"], 1)
            link(dve.tensor_scalar(var, ps[:, 5:7, :].rearrange("p k (l b) -> p (k l) b", b=NB), SCALE * SCALE, EPS,
                                   ALU.mult, ALU.add))
            dve.reciprocal(tmp, var).then_inc(s["chv"], 1)
            dve.wait_ge(s["act_set"], 1)
            link(dve.tensor_tensor(tmp, dall, dall, ALU.mult))
            link(dve.tensor_tensor(tmp, tmp, var, ALU.mult))
            link(dve.tensor_scalar(tmp, tmp, -0.5 * SCALE, 1.5 * SCALE, ALU.mult, ALU.add))
            link(dve.tensor_tensor(dall, dall, tmp, ALU.mult))
            link(dve.reciprocal(tmp, dall))

            sv = sall.rearrange("p (k l) b -> p k l b", l=NLAY)
            dv = dall.rearrange("p (k l) b -> p k l b", l=NLAY)
            iv = tmp.rearrange("p (k l) b -> p k l b", l=NLAY)
            bi = vec[:, NL:2 * NL].rearrange("p (k l) -> p k l", l=NLAY)
            T = {n: t[:, :, :] for n, t in tab.items()}
            dve.tensor_copy(T["S0"], sv[:, :, 0, :])
            dve.tensor_tensor(T["T1"], dv[:, :, 0, :], dv[:, :, 1, :], ALU.mult)
            dve.tensor_tensor(T["bz"], iv[:, :, 0, :], bc(bi[:, :, 0], NB), ALU.mult)
            dve.tensor_tensor(T["E1"], sv[:, :, 2, :], sv[:, :, 1, :], ALU.mult)
            dve.tensor_tensor(T["E2"], sv[:, :, 3, :], dv[:, :, 2, :], ALU.mult)
            dve.tensor_copy(T["D3"], dv[:, :, 3, :])
            dve.tensor_tensor(T["ub"], sv[:, :, 2, :], bc(bi[:, :, 1], NB), ALU.mult)
            link(dve.tensor_tensor(T["sbb"], sv[:, :, 3, :], bc(bi[:, :, 2], NB), ALU.mult))
            link(dve.memset(Bk[:, 0, :], 0.0))
            for k in range(NBLK):
                dve.tensor_scalar(bv[:, 0, :], tab["ub"][0:C, k, :], 2.0, None, ALU.mult).then_inc(s["bv1"], 1)
                dve.wait_ge(s["bp1"], k + 1)
                link(dve.tensor_tensor(bv[:, 1, :], ps[0:C, 0, 0:NB], tab["E2"][0:C, k, :], ALU.mult))
                dve.tensor_tensor(bv[:, 1, :], bv[:, 1, :], tab["sbb"][0:C, k, :], ALU.add).then_inc(s["bv2"], 1)
                dve.wait_ge(s["bp2"], k + 1)
                link(dve.tensor_tensor(tab["c3"][:, k, :], ps[:, 1, 0:NB], tab["D3"][:, k, :], ALU.mult))
                link(dve.tensor_scalar(beta, tab["c3"][:, k, :], vec[:, NL + 4 * k + 3:NL + 4 * k + 4],
                                       None, ALU.add))
                link(dve.tensor_scalar(tab["c3"][:, k, :], tab["c3"][:, k, :], -1.0, None, ALU.mult))
                link(dve.tensor_tensor(Bk[:, k + 1, :], Bk[:, k, :], beta, ALU.add))
                dve.tensor_scalar(nBk[:, k + 1, :], Bk[:, k + 1, :], -1.0, None, ALU.mult).then_inc(s["tabs"], 1)
            for k in range(NBLK):
                for t in range(K):
                    cf = bc(coef[:, :].rearrange("p (j t) -> p j t", t=K)[:, :, t], C)
                    w = wT[:, 4 * k + 1, t, :].unsqueeze(1).broadcast_to([128, NJ, C])
                    link(dve.tensor_tensor(rf[t], w, cf, ALU.mult))
                link(dve.tensor_tensor(rf[0], rf[0], rf[1], ALU.add))
                link(dve.tensor_tensor(rf[0], rf[0], rf[2], ALU.add))
                link(dve.tensor_copy(rh[:, k, :, :], rf[0]))
                ins = dve.tensor_tensor(rl[:, k, :, :], rf[0], rh[:, k, :, :].bitcast(F32), ALU.subtract)
                link(ins)
            dve.memset(gp[:, :, :, :], 0.0).then_inc(s["rt"], NBLK)
            dve.wait_ge(s["z0"], 2)

            def xlo(n):
                st, k, b, sl = where(n)
                dve.wait_ge(s["xhi"], n + 1)
                dve.scalar_tensor_tensor(xl[n % 2][:, 0:XW], X[:, sl, :], Bk[:, k, b:b + 1],
                                         xh[n % 2][:, 0:XW].bitcast(F32), ALU.add, ALU.subtract).then_inc(s["xlo"], 1)

            def zlo(n):
                st, k, b, sl = where(n)
                dve.wait_ge(s["zhi"], n + 1)
                dve.scalar_tensor_tensor(zl[n % 2][:, ZPAD:ZPAD + M], ps[:, ZP + n % 2, :], tab["bz"][:, k, b:b + 1],
                                         zh[n % 2][:, ZPAD:ZPAD + M].bitcast(F32), ALU.add, ALU.subtract) \
                    .then_inc(s["zlo"], 1)

            def xnew(n):
                st, k, b, sl = where(n)
                dve.wait_ge(s["convg"], n + 1)
                dve.wait_ge(s["en"], st + 1)
                o = ps[:, OP + n % 2, :]
                if k < NBLK - 1:
                    dve.scalar_tensor_tensor(X[:, sl, 1:M], o[:, 1:M], tab["D3"][:, k, b:b + 1], X[:, sl, 1:M],
                                             ALU.mult, ALU.add).then_inc(s["xnew"], 1)
                    return
                dve.wait_ge(s["xb"], b + 1)
                j = b // 2
                if j >= 2:
                    dve.wait_ge(s_out[j % 2], 16 * (j // 2))
                t = ot[j % 2][(b % 2) * C:(b % 2 + 1) * C, :]
                dve.scalar_tensor_tensor(t[:, 3:L - 1:2], o[0:C, 2:M], tab["D3"][0:C, k, b:b + 1], X[0:C, sl, 2:M],
                                         ALU.mult, ALU.add)
                dve.scalar_tensor_tensor(t[:, 2:L - 2:2], o[C:128, 1:M - 1], tab["D3"][C:128, k, b:b + 1],
                                         X[C:128, sl, 1:M - 1], ALU.mult, ALU.add).then_inc(s["xnew"], 1)

            def vfull(q):
                st, k, b, sl = where(q * QS)
                dve.wait_ge(s["V"], q + 1)
                if q >= 1:
                    dve.wait_ge(s["vl"], q)
                e = tab["E1"][:, k, b:b + QS].unsqueeze(1).unsqueeze(3).broadcast_to([128, 3, QS, C])
                pv = ps[:, VG:VG + 2, :].rearrange("p k (o s c) -> p (k o) s c", s=QS, c=C)[:, 0:3]
                dve.tensor_tensor(vf[:, :, :, :], pv, e, ALU.mult).then_inc(s["vf"], 1)

            def vlo(q):
                dve.wait_ge(s["vh"], q + 1)
                dve.tensor_tensor(vl[:, :, :, :], vf[:, :, :, :], vh[:, :, :, :].bitcast(F32),
                                  ALU.subtract).then_inc(s["vl"], 1)

            def gplace(q, part):
                st, k, b, sl = where(q * QS)
                if part == 0:
                    dve.wait_ge(s["G"], q + 1)
                    if q >= 1:
                        dve.wait_ge(s["gl"], 2 * q)
                pg = ps[:, VG:VG + 2, :].rearrange("p k (o s c) -> p s (k o) c", s=QS, c=C)
                for row in ((0, 1), (0, 1))[part]:
                    if part == 0:
                        src, dst = pg[0:C], gp[row * C:row * C + C, :, row:8:2, :]
                        t1, ns = tab["T1"][0:C, k, b:b + QS], 4
                    else:
                        src, dst = pg[C:128, :, 1:4], gp[row * C:row * C + C, :, 1 + row:6 + row:2, :]
                        t1, ns = tab["T1"][C:128, k, b:b + QS], 3
                    t1 = t1.unsqueeze(2).unsqueeze(3).broadcast_to([C, QS, ns, C])
                    ins = dve.tensor_tensor(dst, src, t1, ALU.mult)
                if part == 1:
                    ins.then_inc(s["gp"], 1)

            def edge(st, stage):
                g, k = STEPS[st]
                b = g * GS
                base = ps[0:C, EP + stage % 2, :]

                def t(name, n):
                    return tab[name][0:C, k, b:b + GS].unsqueeze(2).unsqueeze(3).broadcast_to([C, GS, 2, n])

                if stage == 0:
                    dve.wait_ge(s["zE"], st + 1)
                    dve.tensor_tensor(ze[:, :, :, 1:6], base[:, 0:GS * 10].rearrange("p (s e t) -> p s e t", s=GS, e=2),
                                      t("bz", 5), ALU.add).then_inc(s["zv"], 1)
                elif stage == 1:
                    dve.wait_ge(s["uE"], st + 1)
                    dve.tensor_tensor(ue[:, :, :, 1:12:2], base[:, 0:GS * 12].rearrange("p (s e t) -> p s e t", s=GS, e=2),
                                      t("E1", 6), ALU.mult)
                    dve.tensor_tensor(ue[:, :, :, 2:12:2], base[:, GS * 12:GS * 22].rearrange("p (s e t) -> p s e t", s=GS, e=2),
                                      t("E1", 5), ALU.mult).then_inc(s["uv"], 1)
                elif stage == 2:
                    dve.wait_ge(s["sE"], st + 1)
                    sv_ = base[:, 0:GS * 12].rearrange("p (s e t) -> p s e t", s=GS, e=2)
                    for e in range(2):
                        ins = dve.scalar_tensor_tensor(se[:, :, e, 2 - 2 * e:8 - 2 * e], sv_[:, :, e, :], 0.25,
                                                       tab["E2"][0:C, k, b:b + GS].unsqueeze(2).broadcast_to([C, GS, 6]),
                                                       ALU.mult, ALU.mult)
                    ins.then_inc(s["sv"], 1)
                else:
                    dve.wait_ge(s["oE"], st + 1)
                    o = ps[:, EP + 1, 0:GS * 4].rearrange("p (s t) -> p s t", s=GS)
                    dve.scalar_tensor_tensor(oe[:, :, :, :].rearrange("p s e t -> p s (e t)"), o, 0.125,
                                             tab["D3"][:, k, b:b + GS].unsqueeze(2).broadcast_to([128, GS, 4]),
                                             ALU.mult, ALU.mult) \
                        .then_inc(s["ov"], 1)

            for stage in range(4):
                edge(0, stage)
            xlo(0)
            for n in range(FIRST, NN):
                if n >= 1:
                    xnew(n - 1)
                if 0 < n + 2 < NN:
                    xlo(n + 2)
                if 0 <= n + 1 < NN:
                    zlo(n + 1)
                if v_at(n - 1) is not None:
                    vlo(v_at(n - 1))
                st, stage = edge_at(n)
                if st is not None:
                    edge(st, stage)
                if v_at(n) is not None:
                    vfull(v_at(n))
                for part in range(2):
                    if g_at(n - part) is not None:
                        gplace(g_at(n - part), part)
            xnew(NN - 1)

        @block.gpsimd
        def _(pool):
            counts, open_ = {}, {}

            def sig(ins, name="chp", by=1):
                ins.then_inc(s[name], by)
                counts[name] = open_[name] = counts.get(name, 0) + by

            def fence():
                for name, n in open_.items():
                    pool.wait_ge(s[name], n)
                open_.clear()

            def link(ins):
                sig(ins)
                fence()

            for r in raw:
                sig(pool.memset(r[0:C, 0:1], 0.0))
                sig(pool.memset(r[0:C, L + 1:L + 2], 0.0))
                fence()
                link(pool.memset(r[C:128, L:L + 2], 0.0))
            for a in (xe, ze, ue, ye, se):
                link(pool.memset(a[:, :, :, :], 0.0))
            sig(pool.memset(w0f[:, :, :, :], 0.0), "z0")
            sig(pool.memset(w3f[:, :, :, :], 0.0))
            link(pool.memset(w2l[:, :, :, :], 0.0))
            pool.wait_ge(s["c_w"], 32 * NBLK)
            wk = wnat.rearrange("p (k l) (i t) -> p k l t i", l=NLAY, t=K)
            for row, slot, tap in ((0, 0, 0), (0, 1, 1), (1, 1, 0), (0, 2, 2), (1, 2, 1), (1, 3, 2)):
                link(pool.tensor_copy(w2l[row * C:row * C + C, :, slot, :], wk[:, :, 2, tap, :]))
            pool.wait_ge(s["e2"], 6)
            wv = wT[:, :, :, :].rearrange("p (k l) t c -> p k l t c", l=NLAY)
            for row, slot, tap in ((0, 0, 0), (0, 2, 2), (0, 3, 1), (1, 0, 1), (1, 1, 0), (1, 3, 2)):
                h = slice(row * C, row * C + C)
                link(pool.tensor_copy(w0f[h, :, slot, :], wv[h, :, 0, tap, :]))
            for row, slot, tap in ((0, 0, 0), (0, 1, 2), (1, 0, 1)):
                h = slice(row * C, row * C + C)
                link(pool.tensor_copy(w3f[h, :, slot, :], wv[h, :, 3, tap, :]))
            for a in (zh[0], zh[1], zl[0], zl[1]):
                link(pool.memset(a[:, :].bitcast(F32), 0.0))
            sig(pool.memset(en[:, :, :, :], 0.0), "z0")
            pool.wait_ge(s["tabs"], NBLK)
            pool.wait_ge(s["rt"], NBLK)

            def xcopy(b):
                pool.wait_ge(s_raw[b % 2], 32 * (b // 2 + 1))
                if b >= NR * GS:
                    pool.wait_ge(s["xnew"], nth(b - NR * GS, NBLK - 1) + 1)
                sl = (b // GS % NR) * GS + b % GS
                sig(pool.tensor_copy(X[:, sl, :], raw[b % 2][:, 0:2 * XW:2]), "xcopy")

            def w3s(q):
                st, k, b, sl = where(q * QS)
                if q >= 1:
                    pool.wait_ge(s["V"], q)
                e = tab["E2"][:, k, b:b + QS].unsqueeze(1).unsqueeze(3).broadcast_to([128, 2, QS, C])
                w = w3f[:, k, :, :].unsqueeze(2).broadcast_to([128, 2, QS, C])
                sig(pool.tensor_tensor(w3q[:, :, :, :], w, e, ALU.mult), "w3q")

            def w0lo(q):
                pool.wait_ge(s["w0h"], q + 1)
                sig(pool.tensor_tensor(w0l[q % 2][:, :, :], w0q[:, :, :], w0h[q % 2][:, :, :].bitcast(F32),
                                   ALU.subtract), "w0l")

            def glo(q):
                for j, h in enumerate((slice(0, 2), slice(2, 4))):
                    pool.wait_ge(s["gh"], 2 * q + 1 + j)
                    sig(pool.tensor_tensor(gl[q % 2][:, h, :, :], gp[:, h, :, :], gh[q % 2][:, h, :, :].bitcast(F32),
                                           ALU.subtract), "gl")

            def x_ends(st):
                g, k = STEPS[st]
                return X[:, (g % NR) * GS:(g % NR + 1) * GS, :]

            def edge_x(st):
                g, k = STEPS[st]
                b = g * GS
                if k == 0:
                    pool.wait_ge(s["xcopy"], b + GS)
                else:
                    pool.wait_ge(s["xnew"], GS * (st - 1))
                    pool.wait_ge(s["eap"], st - 1)
                if st >= 1:
                    pool.wait_ge(s["zE"], st)
                xv = x_ends(st)
                for e in range(2):
                    lo, hi = (slice(1, 4), slice(0, 3)) if e == 0 else (slice(M - 2, M + 1), slice(M - 3, M))
                    at = 1 - e
                    sig(pool.tensor_tensor(xe[:, :, e, at + 1:at + 6:2], xv[0:C, :, lo],
                                       Bk[0:C, k, b:b + GS].unsqueeze(2).broadcast_to([C, GS, 3]), ALU.add))
                    fence()
                    link(pool.tensor_tensor(xe[:, :, e, at:at + 5:2], xv[C:128, :, hi],
                                            Bk[C:128, k, b:b + GS].unsqueeze(2).broadcast_to([C, GS, 3]), ALU.add))
                xf = xe[:, :, :, :].rearrange("p s e t -> p s (e t)")
                sig(pool.tensor_tensor(xf, xf, tab["S0"][0:C, k, b:b + GS].unsqueeze(2).broadcast_to([C, GS, 14]),
                                   ALU.mult), "xe")

            def edge_z(st):
                g, k = STEPS[st]
                b = g * GS
                pool.wait_ge(s["zv"], st + 1)
                zf = ze[:, :, :, :].rearrange("p s e t -> p s (e t)")
                sig(pool.tensor_tensor(zf, zf, tab["T1"][0:C, k, b:b + GS].unsqueeze(2).broadcast_to([C, GS, 14]),
                                   ALU.mult), "ze")

            def blur(dst, src, n, off, last, name):
                a1, a2 = b1[:, :, :, 0:n + 2], b2[:, :, :, 0:n + 1]
                for e in range(2):
                    o = off[e]
                    ins = pool.tensor_tensor(a1[:, :, e, :], src[:, :, e, o:o + n + 2], src[:, :, e, o + 1:o + n + 3], ALU.add)
                    sig(ins)
                fence()
                link(pool.tensor_tensor(a2, b1[:, :, :, 0:n + 1], b1[:, :, :, 1:n + 2], ALU.add))
                for e in range(2):
                    o = last[e]
                    ins = pool.tensor_tensor(dst[:, :, e, o:o + n], b2[:, :, e, 0:n], b2[:, :, e, 1:n + 1], ALU.add)
                    sig(ins, name if e else "chp")

            def edge_u(st):
                g, k = STEPS[st]
                b = g * GS
                pool.wait_ge(s["uv"], st + 1)
                uv = ue[:, :, :, 1:12]
                link(pool.tensor_tensor(uv, uv, tab["ub"][0:C, k, b:b + GS].unsqueeze(2).unsqueeze(3)
                                        .broadcast_to([C, GS, 2, 11]), ALU.add))
                blur(ye, ue, 7, (0, 3), (1, 0), "ye")

            def edge_s(st):
                g, k = STEPS[st]
                b = g * GS
                pool.wait_ge(s["sv"], st + 1)
                for e in range(2):
                    sv_ = se[:, :, e, 2 - 2 * e:8 - 2 * e]
                    ins = pool.tensor_tensor(sv_, sv_, tab["sbb"][0:C, k, b:b + GS].unsqueeze(2).broadcast_to([C, GS, 6]), ALU.add)
                    sig(ins)
                fence()
                blur(ve, se, 5, (0, 0), (0, 0), "ve")

            def edge_o(st):
                g, k = STEPS[st]
                b = g * GS
                xv = x_ends(st)
                pool.wait_ge(s["ov"], st + 1)
                of = oe[:, :, :, :].rearrange("p s e t -> p s (e t)")
                link(pool.tensor_tensor(of, of, tab["c3"][:, k, b:b + GS].unsqueeze(2).broadcast_to([128, GS, 4]), ALU.add))
                ev = en[:, st % 2, :, :]
                sig(pool.tensor_tensor(ev[0:C], oe[0:C, :, :, 1], xv[0:C, :, 1:M + 1:M - 1], ALU.add))
                fence()
                ins = pool.tensor_tensor(ev[C:128], oe[C:128, :, :, 0], xv[C:128, :, 0:M:M - 1], ALU.add)
                if k == NBLK - 1:
                    link(ins)
                    ins = pool.tensor_tensor(ev, ev, Bk[:, NBLK, b:b + GS].unsqueeze(2).broadcast_to([128, GS, 2]), ALU.add)
                sig(ins, "en")
                fence()

            def edge_apply(st):
                g, k = STEPS[st]
                b = g * GS
                pool.wait_ge(s["xnew"], GS * (st + 1))
                xv, ev = x_ends(st), en[:, st % 2, :, :]
                fence()
                if k < NBLK - 1:
                    link(pool.tensor_copy(xv[C:128, :, 0:M:M - 1], ev[C:128]))
                    link(pool.tensor_copy(xv[C:128, :, M], nBk[C:128, k + 1, b:b + GS]))
                    sig(pool.tensor_copy(xv[0:C, :, 1:M + 1:M - 1], ev[0:C]))
                    sig(pool.tensor_copy(xv[0:C, :, 0], nBk[0:C, k + 1, b:b + GS]), "eap")
                else:
                    sig(pool.memset(b1[:, 0, 0, 0:1], 0.0), "eap")
                fence()

            def finish(n):
                st, k, b, sl = where(n)
                pool.wait_ge(s["xlo"], n + 1)
                pool.wait_ge(s["en"], st + 1)
                sig(pool.tensor_scalar(X[:, sl, :], X[:, sl, :], Bk[:, NBLK, b:b + 1], None, ALU.add), "xb")
                j = b // 2
                if j >= 2:
                    pool.wait_ge(s_out[j % 2], 16 * (j // 2))
                t = ot[j % 2][(b % 2) * C:(b % 2 + 1) * C, :]
                ev = en[:, st % 2, b % GS, :]
                fence()
                link(pool.tensor_copy(t[:, 0:L - 1:L - 2], ev[C:128]))
                sig(pool.tensor_copy(t[:, 1:L:L - 2], ev[0:C]), "oed")
                fence()

            for b in range(2 * GS):
                xcopy(b)
                if b == GS - 1:
                    edge_x(0)
                    edge_z(0)
                    edge_u(0)
                    edge_s(0)
                    edge_o(0)
            w3s(0)
            for n in range(FIRST, NN):
                st, i = divmod(n, GS)
                if n >= 0:
                    if STEPS[st][1] == NBLK - 1:
                        finish(n)
                    if loads_at(n) is not None:
                        xcopy(loads_at(n))
                if n >= 1 and n % GS == 1 and st >= 1:
                    edge_apply(st - 1)
                if g_at(n) is not None:
                    w0lo(g_at(n))
                if n >= 0 and st + 1 < NS:
                    for at, stage in ((2, edge_x), (3, edge_z), (4, edge_u), (6, edge_s), (7, edge_o)):
                        if i == at:
                            stage(st + 1)
                if g_at(n - 2) is not None:
                    glo(g_at(n - 2))
                if v_at(n + 2) is not None and v_at(n + 2) > 0:
                    w3s(v_at(n + 2))


def kernel(**inputs):
    import concourse.bacc as bacc
    from concourse.bass_utils import run_bass_kernel_spmd

    nc = bacc.Bacc("TRN2", target_bir_lowering=False, num_devices=1)
    arrays = {}

    def dram(name, a):
        a = np.ascontiguousarray(a)
        arrays[name] = a
        return nc.dram_tensor(name, a.shape, mybir.dt.from_np(a.dtype), kind="ExternalInput").ap()

    x = dram("x_in", inputs["x"])
    style = dram("style_in", inputs["cond_512"])
    weights, biases, mod_w, mod_b = (
        [dram(f"{what}{k}_in", inputs[f"L{k}_cond_{what}"]) for k in range(NBLK)]
        for what in ("weights", "biases", "mod_w", "mod_b"))
    ident_d = dram("ident_in", np.eye(128, dtype=np.float32))
    coef_d = dram("coef_in", blur_table())
    out = nc.dram_tensor("out_x", (NB, C, L), F32, kind="ExternalOutput").ap()
    build(nc, x, style, weights, biases, mod_w, mod_b, ident_d, coef_d, out)
    r = run_bass_kernel_spmd(nc, [arrays], core_ids=[0])
    return r.results[0]["out_x"]
```

```python
from contextlib import ExitStack

import numpy as np

import concourse.bass as bass
from concourse import mybir

F32 = mybir.dt.float32
F32R = mybir.dt.float32r
ALU = mybir.AluOpType
ACT = mybir.ActivationFunctionType
IDENT = ACT.Identity

NB, C, L, SD = 64, 64, 1024, 128
NBLK, NLAY, K = 4, 4, 3
NL = NBLK * NLAY
SCALE = 1.0 / float(np.sqrt(C * K ** 2))
EPS = 1e-8
M = L // 2
XW = M + 1
ZPAD = 2
GS = 8
NG = NB // GS
NR = 3
QS = 4
STEPS = [(2 * (p // (2 * NBLK)) + p % 2, (p // 2) % NBLK) for p in range(NG * NBLK)]
NS = len(STEPS)
NN = NS * GS
NQ = NN // QS
V_LEAD, G_LEAD = 6, 4
EDGE_SLOTS = (3, 4, 6, 7)
TRANSPOSE, STYLE, DEMOD, NEWTON, TABLES, BIAS_U, BIAS_S, SPLIT_W2, R_TAP0, R_TAP1, R_TAP2, SPLIT_R = range(12)
SETUP_SLOTS = {0: (TRANSPOSE,), 1: (STYLE,), 2: (DEMOD,), 3: (NEWTON,), 4: (TABLES,), 5: (BIAS_U, R_TAP0),
               6: (SPLIT_W2, R_TAP1), 7: (R_TAP2,), 9: (BIAS_S,), 10: (SPLIT_R,)}
FIRST_COPIES = {-6: (2, 6), -5: (6, 8), -3: (8, 10), -2: (10, 12), -1: (12, 14), 0: (14, 16)}
LT = {0: 0, 2: 1, 3: 2}
NJ = 7
ALLBLUR = [1, 6, 15, 20, 15, 6, 1]
ZP, OP, VG, EP = 0, 2, 4, 6


def blur_table():
    t = np.zeros((2 * C, NJ * K), np.float32)
    for half in range(2):
        for j in range(NJ):
            for c in range(K):
                i = 2 * j - 8 - half + 4 + c
                if -6 <= 2 * j - 8 - half <= 2 and 0 <= i < 7:
                    t[half * C:(half + 1) * C, j * K + c] = ALLBLUR[i] / 32.0
    return t


def build(nc, x, style, weights, biases, mod_w, mod_b, ident_d, coef_d, out):
    ctx = ExitStack()
    with ctx:
        def sb(name, shape, dt=F32):
            return ctx.enter_context(nc.sbuf_tensor(name, shape, dt))

        def sem(name):
            return ctx.enter_context(nc.semaphore(name))

        ps = ctx.enter_context(nc.psum_tensor("ps", [128, 8, 512], F32))

        wT = sb("wT", [128, NBLK, 3, K, C])
        w1nat = sb("w1nat", [C, NBLK, C * K])
        w0f = sb("w0f", [128, NBLK, 4, C])
        w3f = sb("w3f", [128, NBLK, 2, C])
        w2h = sb("w2h", [128, NBLK, 4, C], F32R)
        w2l = sb("w2l", [128, NBLK, 4, C], F32R)
        w2d = sb("w2d", [128, NBLK, 4, C], F32R)
        rh = sb("rh", [128, NBLK, NJ, C], F32R)
        rl = sb("rl", [128, NBLK, NJ, C], F32R)
        rd = sb("rd", [128, NBLK, NJ - 2, C], F32R)
        names = ["S0", "T1", "bz", "E1", "E2", "D3", "ub", "sbb", "c3"]
        tab = {n: sb(f"t_{n}", [128, NBLK, NB]) for n in names}
        Bk = sb("Bk", [128, NBLK + 1, NB])

        X = sb("X", [128, NR * GS, XW])
        raw = [sb(f"raw{i}", [128, 2 * XW]) for i in range(2)]
        ot = [sb(f"ot{i}", [128, L]) for i in range(2)]
        xh = [sb(f"xh{i}", [128, XW + 1], F32R) for i in range(2)]
        xl = [sb(f"xl{i}", [128, XW + 1], F32R) for i in range(2)]
        zh = [sb(f"zh{i}", [128, M + 4], F32R) for i in range(2)]
        zl = [sb(f"zl{i}", [128, M + 4], F32R) for i in range(2)]
        w0h = [sb(f"w0h{i}", [128, QS, 4 * C], F32R) for i in range(2)]
        w0l = [sb(f"w0l{i}", [128, QS, 4 * C], F32R) for i in range(2)]
        w3q = sb("w3q", [128, 2, QS, C])
        w3h = sb("w3h", [128, 2, QS, C], F32R)
        w3l = sb("w3l", [128, QS, C], F32R)
        vf = sb("vf", [128, 3, QS, C])
        vh = sb("vh", [128, 3, QS, C], F32R)
        vl = sb("vl", [128, 2, QS, C], F32R)
        gp = sb("gp", [128, QS, 8, C])
        gh = [sb(f"gh{i}", [128, QS // 2, 8, C], F32R) for i in range(3)]
        gl = [sb(f"gl{i}", [128, QS // 2, 8, C], F32R) for i in range(3)]
        xe = sb("xe", [C, GS, 2, 7])
        ze = sb("ze", [C, GS, 2, 7])
        ue = sb("ue", [C, GS, 2, 13])
        b1 = sb("b1", [C, GS, 2, 9])
        b2 = sb("b2", [C, GS, 2, 8])
        ye = sb("ye", [C, GS, 2, 8])
        se = sb("se", [C, GS, 2, 8])
        ve = sb("ve", [C, GS, 2, 5])
        oe = sb("oe", [128, GS, 2, 2])
        en = sb("en", [128, 2, GS, 2])

        def xcols(lo, n):
            return X[:, 2 * GS:3 * GS, :].rearrange("p s m -> p (s m)")[:, lo:lo + n]

        LC = NLAY * C
        wnat = xcols(0, NL * C * K)[0:C].rearrange("p (l w) -> p l w", l=NL)
        wsq = xcols(0, LC * K)[C:128].rearrange("p (l t c) -> p l t c", l=NLAY, t=K)
        wsum = wsq[:, :, 0, :]
        ssq = xcols(LC * K, LC)[C:128].rearrange("p (l b) -> p l b", l=NLAY)
        sall, dall, var, tmp = (xcols(NL * C * K + i * LC, LC).rearrange("p (l b) -> p l b", l=NLAY) for i in range(4))
        mwn = ot[0][:, :].rearrange("p (l d) -> p l d", l=NL // 2)
        mwT = ot[0][:, :].rearrange("p (l c) -> p l c", l=NL)
        rf = [ot[1][:, i * NJ * C:(i + 1) * NJ * C].rearrange("p (j c) -> p j c", j=NJ) for i in range(2)]
        ident = ot[1][:, 2 * NJ * C:2 * NJ * C + 128]
        style_n = ot[1][0:NB, 0:SD]
        vecn = ot[1][0:2 * NL, SD:SD + C]
        misc = sb("misc", [128, 2 * NB + 2 * NL + NJ * K])
        w1T = sb("w1T", [128, K, C])
        styleT = misc[:, 0:NB]
        beta = misc[:, NB:2 * NB]
        vec = misc[:, 2 * NB:2 * NB + 2 * NL]
        coef = misc[:, 2 * NB + 2 * NL:2 * NB + 2 * NL + NJ * K]
        bv = xcols(LC * K + LC, 2 * NB)[C:128].rearrange("p (i b) -> p i b", i=2)

        s = {n: sem(f"s_{n}") for n in [
            "c_small", "tr0", "vec",
            "tr", "wT", "w03", "w2h", "w2l", "rt",
            "Sp", "sq", "Dp", "var", "rcp", "sqrt",
            "bv1", "bp1", "bv2", "bp2", "tabs",
            "z0",
            "xcopy", "xhi", "xlo", "conv0", "zhi", "zlo", "convg", "xnew",
            "xb", "oed",
            "w3q", "w3h", "w3l", "w0h", "w0l", "V", "vf", "vh", "vl", "G", "gp", "gh", "gl",
            "xe", "zE", "zv", "ze", "uE", "uv", "ye", "sE", "sv", "ve", "oE", "ov", "en",
            "eap",
            "dve_set", "chp"]}
        s_w = [sem(f"s_w{k}") for k in range(NBLK)]
        s_raw = [sem(f"s_raw{i}") for i in range(2)]
        s_out = [sem(f"s_out{i}") for i in range(2)]

        def where(n):
            st, i = divmod(n, GS)
            g, k = STEPS[st]
            return st, k, g * GS + i, (g % NR) * GS + i

        def nth(b, k):
            g, i = divmod(b, GS)
            return STEPS.index((g, k)) * GS + i

        def loads_at(n):
            st, i = divmod(n, GS)
            if st + 2 < NS and STEPS[st + 2][1] == 0 and STEPS[st + 2][0] >= 2:
                return STEPS[st + 2][0] * GS + i
            return None

        def v_at(n):
            q, i = divmod(n + V_LEAD, QS)
            return q if i == 0 and 0 <= q < NQ else None

        def g_at(n):
            q, i = divmod(n + G_LEAD, QS)
            return q if i == 0 and 0 <= q < NQ else None

        def edge_at(n):
            st, i = divmod(n, GS)
            if -4 <= n < 0:
                return 0, n + 4
            return (st + 1, EDGE_SLOTS.index(i)) if n >= 0 and i in EDGE_SLOTS and st + 1 < NS else (None, None)

        def setup_at(n):
            if n < -4:
                return 0, ((BIAS_U,) if n == FIRST else (BIAS_S,))
            k, i = n // (2 * GS) + 1, n % (2 * GS)
            return (k, SETUP_SLOTS.get(i, ())) if 0 <= n and k < NBLK else (None, ())

        FIRST = -V_LEAD
        block = ctx.enter_context(nc.Block())

        def load_weights(engine, k):
            engine.dma_start(mwn[:, 2 * k:2 * k + 2, :],
                             mod_w[k].rearrange("(a l) c d -> (l c) a d", l=2)).then_inc(s_w[k], 16)
            engine.dma_start(wnat[:, 4 * k:4 * k + 4, :], weights[k].rearrange("l o i t -> o l (i t)")).then_inc(s_w[k], 16)
            engine.dma_start(w1nat[:, k, :], weights[k][1].rearrange("o i t -> o (i t)")).then_inc(s_w[k], 16)

        @block.sync
        def _(sp):
            def load(b):
                r = raw[b % 2]
                if b >= 2:
                    sp.wait_ge(s["xcopy"], b - 1)
                else:
                    sp.wait_ge(s["z0"], 1)
                sp.dma_start(r[0:C, 1:L + 1], x[b]).then_inc(s_raw[b % 2], 16)
                sp.dma_start(r[C:128, 0:L], x[b]).then_inc(s_raw[b % 2], 16)

            def store(j):
                n = nth(2 * j + 1, NBLK - 1)
                sp.wait_ge(s["xnew"], n + 1)
                sp.wait_ge(s["oed"], 2 * j + 2)
                sp.dma_start(out[2 * j:2 * j + 2].rearrange("b c t -> (b c) t"), ot[j % 2][:, :]) \
                    .then_inc(s_out[j % 2], 16)

            sp.dma_start(ident, ident_d).then_inc(s["c_small"], 16)
            sp.dma_start(style_n, style).then_inc(s["c_small"], 16)
            for k in range(NBLK):
                sp.dma_start(vecn[4 * k:4 * k + 4, :], mod_b[k]).then_inc(s["c_small"], 16)
                sp.dma_start(vecn[NL + 4 * k:NL + 4 * k + 4, :], biases[k]).then_inc(s["c_small"], 16)
            sp.dma_start(coef, coef_d).then_inc(s["c_small"], 16)
            for b in range(2 * GS):
                load(b)
                if 0 <= b - GS < NBLK - 1:
                    load_weights(sp, b - GS + 1)
            for n in range(NN + 1):
                if n < NN and loads_at(n) is not None:
                    load(loads_at(n))
                if n >= 1 and n % 2 == 0 and where(n - 1)[1] == NBLK - 1:
                    store(where(n - 1)[2] // 2)
            for i in range(2):
                sp.wait_ge(s_out[i], 16 * (NB // 4))

        @block.tensor
        def _(pe):
            fl = ps[:, EP:EP + 2, :].rearrange("p k n -> p (k n)")

            def twice(at, n, a, b, first=True, last=True):
                for h in range(2):
                    m = pe.matmul(fl[h * C:(h + 1) * C, at:at + n], a, b, start=first, stop=last, skip_group_check=True)
                return m

            def setup(k, stage):
                if stage == TRANSPOSE:
                    pe.wait_ge(s_w[k], 48)
                    if k >= 1:
                        pe.wait_ge(s["ov"], 2 * k - 1)
                    for j in range(2):
                        pe.transpose(fl[:, j * 128:j * 128 + 128], mwn[:, 2 * k + j, :], ident)
                    for at, l in enumerate((0, 2, 3, 1)):
                        w = wnat[:, 4 * k + l, :].rearrange("p (i t) -> p i t", t=K)
                        for t in range(K):
                            a = 4 * C + (at * K + t) * C
                            m = twice(a, C, w[:, :, t], ident[0:C, 0:C])
                    m.then_inc(s["tr"], 1)
                elif stage == STYLE:
                    pe.wait_ge(s["wT"], k + 1)
                    for l in range(NLAY):
                        m = twice(l * NB, NB, mwT[:, 4 * k + l, :], styleT)
                    m.then_inc(s["Sp"], 1)
                elif stage == DEMOD:
                    pe.wait_ge(s["sq"], k + 1)
                    for l in range(NLAY):
                        m = twice(512 + l * NB, NB, wsum[:, 3 if l == 1 else LT[l], :], ssq[:, l, :])
                    m.then_inc(s["Dp"], 1)
                elif stage == BIAS_U:
                    pe.wait_ge(s["bv1"], k + 1)
                    for t in range(K):
                        m = pe.matmul(fl[C:128, 0:NB], wT[C:128, k, LT[2], t, :], bv[:, 0, :],
                                      start=(t == 0), stop=(t == K - 1), skip_group_check=True)
                    m.then_inc(s["bp1"], 1)
                elif stage == BIAS_S:
                    pe.wait_ge(s["bv2"], k + 1)
                    if k >= 1:
                        pe.wait_ge(s["ov"], 2 * k)
                    for t in range(K):
                        m = twice(512, NB, wT[C:128, k, LT[3], t, :], bv[:, 1, :], t == 0, t == K - 1)
                    m.then_inc(s["bp2"], 1)

            pe.wait_ge(s["c_small"], (3 + 2 * NBLK) * 16)
            pe.transpose(ps[:, 0, 0:NB], style_n, ident[0:NB, 0:NB])
            for h in range(2):
                m = pe.matmul(ps[h * C:(h + 1) * C, 0, NB:NB + 2 * NL], vecn, ident[0:2 * NL, 0:2 * NL],
                              start=True, stop=True, skip_group_check=True)
            m.then_inc(s["tr0"], 1)
            setup(0, TRANSPOSE)
            pe.wait_ge(s["vec"], 1)
            setup(0, STYLE)
            setup(0, DEMOD)
            pe.wait_ge(s["z0"], 3)

            def products(out_ap, ah, al, bh, bl, first, last):
                pe.matmul(out_ap, ah, bh, start=first, stop=False, skip_group_check=True)
                pe.matmul(out_ap, ah, bl, start=False, stop=False, skip_group_check=True)
                return pe.matmul(out_ap, al, bh, start=False, stop=last, skip_group_check=True)

            def stacked(out_ap, ah, al, b, first, last):
                pe.matmul(out_ap, ah, b, start=first, stop=False, skip_group_check=True)
                return pe.matmul(out_ap, al, b[0:C], start=False, stop=last, skip_group_check=True)

            def conv0(n):
                q, i, b = n // QS, n % QS, n % 2
                pe.wait_ge(s["xlo"], n + 1)
                if i == 0:
                    pe.wait_ge(s["w0l"], q + 1)
                if n >= 2:
                    pe.wait_ge(s["zlo"], n - 1)
                for d in range(2):
                    w = slice(d * 128, d * 128 + 128)
                    m = products(ps[:, ZP + b, :], w0h[q % 2][:, i, w], w0l[q % 2][:, i, w],
                                 xh[b][:, d:d + M], xl[b][:, d:d + M], d == 0, d == 1)
                m.then_inc(s["conv0"], 1)

            def convg(n):
                q, i, b = n // QS, n % QS, n % 2
                pe.wait_ge(s["zlo"], n + 1)
                if i % 2 == 0:
                    pe.wait_ge(s["gl"], 2 * q + 1 + i // 2)
                if n >= 2:
                    pe.wait_ge(s["xnew"], n - 1)
                for j, d in enumerate((1, 0, -1, -2)):
                    c = slice(ZPAD + d, ZPAD + d + M)
                    m = products(ps[:, OP + b, :], gh[n // 2 % 3][:, n % 2, 2 * j:2 * j + 2, :], gl[n // 2 % 3][:, n % 2, 2 * j:2 * j + 2, :],
                                 zh[b][:, c], zl[b][:, c], j == 0, j == 3)
                m.then_inc(s["convg"], 1)

            def v_products(q):
                k = STEPS[q * QS // GS][1]
                pe.wait_ge(s["w3l"], q + 1)
                pe.wait_ge(s["w2l"], k + 1)
                if q >= 1:
                    pe.wait_ge(s["gp"], q)
                a = ps[:, VG, :].rearrange("p (o s c) -> p o s c", o=2, s=QS)
                b = ps[:, VG + 1, 0:QS * C].rearrange("p (s c) -> p s c", s=QS)
                for o, c, first in ((a[:, 0], slice(0, 2), True), (a[:, 1], slice(2, 4), False)):
                    products(o, w2h[:, k, c, :], w2l[:, k, c, :], w3h[:, 0], w3l[:, :, :], first, False)
                for o, c, first in ((a[:, 1], slice(0, 2), False), (b, slice(2, 4), True)):
                    m = stacked(o, w2d[:, k, c, :], w2l[0:C, k, c, :], w3h[:, 1], first, True)
                m.then_inc(s["V"], 1)

            def g_products(q):
                k = STEPS[q * QS // GS][1]
                pe.wait_ge(s["vl"], q + 1)
                pe.wait_ge(s["rt"], k + 1)
                seen = set()
                for jw in range(NJ - 1):
                    for sg in range(4):
                        for o in range(3):
                            if 4 * sg - 2 * o - 6 != 2 * jw - 8:
                                continue
                            sr = 3 - sg
                            bank, at = VG + sr // 2, (sr % 2) * QS * C
                            first = bank not in seen
                            if o < 2:
                                m = products(ps[:, bank, at:at + QS * C],
                                             rh[:, k, jw:jw + 2, :], rl[:, k, jw:jw + 2, :],
                                             vh[:, o, :, :], vl[:, o, :, :], first, False)
                            else:
                                w = 2 if sg < 3 else 1
                                m = stacked(ps[0:w * C, bank, at:at + QS * C],
                                            rd[:, k, jw - 1:jw - 1 + w, :], rl[0:C, k, jw:jw + w, :],
                                            vh[:, 2, :, :], first, False)
                            seen.add(bank)
                m.then_inc(s["G"], 1)

            def edge(st, stage):
                k = STEPS[st][1]
                bank = EP + stage % 2
                started = min(NBLK, (st - 1) // 2 + 2)
                if stage < 3:
                    pe.wait_ge(s[("sq", "tabs" if st % 2 == 0 else "var", "bv2")[stage]], started)
                base = ps[0:C, bank, :]
                if stage == 0:
                    pe.wait_ge(s["xe"], st + 1)
                    o = base[:, 0:GS * 10].rearrange("p (s e t) -> p s e t", s=GS, e=2)
                    for t in range(K):
                        m = pe.matmul(o, wT[0:C, k, LT[0], t, :], xe[:, :, :, t:t + 5], start=(t == 0), stop=(t == K - 1),
                                      skip_group_check=True)
                    m.then_inc(s["zE"], 1)
                elif stage == 1:
                    pe.wait_ge(s["ze"], st + 1)
                    even = base[:, 0:GS * 12].rearrange("p (s e t) -> p s e t", s=GS, e=2)
                    odd = base[:, GS * 12:GS * 22].rearrange("p (s e t) -> p s e t", s=GS, e=2)
                    w1 = w1nat[:, k, :].rearrange("p (i t) -> p i t", t=K)
                    pe.matmul(even, w1[:, :, 0], ze[:, :, :, 1:7], start=True, stop=False, skip_group_check=True)
                    pe.matmul(even, w1[:, :, 2], ze[:, :, :, 0:6], start=False, stop=True, skip_group_check=True)
                    pe.matmul(odd, w1[:, :, 1], ze[:, :, :, 1:6], start=False, stop=True,
                              skip_group_check=True).then_inc(s["uE"], 1)
                elif stage == 2:
                    pe.wait_ge(s["ye"], st + 1)
                    o = base[:, 0:GS * 12].rearrange("p (s e t) -> p s e t", s=GS, e=2)
                    for t in range(K):
                        m = pe.matmul(o, wT[0:C, k, LT[2], t, :], ye[:, :, :, t:t + 6], start=(t == 0),
                                      stop=(t == K - 1), skip_group_check=True)
                    m.then_inc(s["sE"], 1)
                else:
                    pe.wait_ge(s["ve"], st + 1)
                    for h in range(2):
                        o = ps[h * C:(h + 1) * C, bank, 0:GS * 4].rearrange("p (s e t) -> p s e t", s=GS, e=2)
                        for t in range(K):
                            m = pe.matmul(o, wT[0:C, k, LT[3], t, :], ve[:, :, :, t:t + 3:2], start=(t == 0),
                                          stop=(t == K - 1), skip_group_check=True)
                    m.then_inc(s["oE"], 1)

            for n in range(FIRST, NN):
                if 0 < n + 1 < NN or n == -2:
                    conv0(max(n + 1, 0))
                k, stages = setup_at(n)
                for stage in stages:
                    setup(k, stage)
                if g_at(n) is not None:
                    g_products(g_at(n))
                st, stage = edge_at(n)
                if st is not None and stage < 3:
                    edge(st, stage)
                if n >= 0:
                    convg(n)
                if st is not None and stage == 3:
                    edge(st, stage)
                if v_at(n) is not None:
                    v_products(v_at(n))

        @block.scalar
        def _(act):
            load_weights(act, 0)
            fl = ps[:, EP:EP + 2, :].rearrange("p k n -> p (k n)")

            def xcopy(b):
                act.wait_ge(s_raw[b % 2], 32 * (b // 2 + 1))
                if b >= NR * GS:
                    last = nth(b - NR * GS, NBLK - 1)
                    act.wait_ge(s["xnew"], last + 1)
                    act.wait_ge(s["eap"], last // GS)
                sl = (b // GS % NR) * GS + b % GS
                act.activation(X[:, sl, :], raw[b % 2][:, 0:2 * XW:2], ACT.Copy).then_inc(s["xcopy"], 1)

            def setup(k, stage):
                if stage == TRANSPOSE:
                    act.wait_ge(s["tr"], k + 1)
                    act.wait_ge(s["rt"], k)
                    act.activation(mwT[:, 4 * k:4 * k + 4, :].rearrange("p l c -> p (l c)"), fl[:, 0:4 * C], ACT.Copy)
                    act.activation(wT[:, k, :, :, :].rearrange("p l t c -> p (l t c)"), fl[:, 4 * C:4 * C + 3 * K * C], ACT.Copy)
                    act.activation(w1T[:, :, :].rearrange("p t c -> p (t c)"), fl[:, 4 * C + 3 * K * C:16 * C],
                                   ACT.Copy).then_inc(s["wT"], 1)
                elif stage == STYLE:
                    act.wait_ge(s["wT"], k + 1)
                    if k == 0:
                        act.wait_ge(s["z0"], 2)
                    lo, hi = slice(0, C), slice(C, 128)
                    for h, dst, l, t in ((lo, w0f[:, k, 0], 0, 0), (lo, w0f[:, k, 2], 0, 2), (lo, w0f[:, k, 3], 0, 1),
                                         (hi, w0f[:, k, 0], 0, 1), (hi, w0f[:, k, 1], 0, 0), (hi, w0f[:, k, 3], 0, 2),
                                         (lo, w3f[:, k, 0], 3, 0), (lo, w3f[:, k, 1], 3, 2), (hi, w3f[:, k, 0], 3, 1),
                                         (hi, w3f[:, k, 1], 3, 2)):
                        ins = act.activation(dst[h], wT[h, k, LT[l], t, :], ACT.Copy)
                    ins.then_inc(s["w03"], 1)
                    w = wnat[:, 4 * k + 2, :].rearrange("p (i t) -> p t i", t=K)
                    for dst in (w2h[lo, k, 0:3], w2h[hi, k, 1:4], w2d[lo, k, 0:3], w2d[hi, k, 0:3]):
                        ins = act.activation(dst, w, ACT.Copy)
                    ins.then_inc(s["w2h"], 1)
                elif stage == DEMOD:
                    act.wait_ge(s["rcp"], k + 1)
                    act.activation(dall, tmp, ACT.Sqrt).then_inc(s["sqrt"], 1)

            setup(0, TRANSPOSE)
            setup(0, STYLE)
            xcopy(0)
            xcopy(1)
            setup(0, DEMOD)
            act.wait_ge(s["z0"], 3)

            def xhi(n):
                st, k, b, sl = where(n)
                if k == 0:
                    act.wait_ge(s["xcopy"], b + 1)
                else:
                    act.wait_ge(s["xnew"], n - 2 * GS + 1)
                    act.wait_ge(s["eap"], st - 1)
                    act.wait_ge(s["tabs"], k)
                if n >= 2:
                    act.wait_ge(s["conv0"], n - 1)
                act.activation(xh[n % 2][:, 0:XW], X[:, sl, :], IDENT, bias=Bk[:, k, b:b + 1]).then_inc(s["xhi"], 1)

            def zhi(n):
                st, k, b, sl = where(n)
                act.wait_ge(s["conv0"], n + 1)
                if n >= 2:
                    act.wait_ge(s["convg"], n - 1)
                act.activation(zh[n % 2][:, ZPAD:ZPAD + M], ps[:, ZP + n % 2, :], IDENT,
                               bias=tab["bz"][:, k, b:b + 1]).then_inc(s["zhi"], 1)

            def xb(n):
                st, k, b, sl = where(n)
                act.wait_ge(s["xlo"], n + 1)
                act.wait_ge(s["en"], st + 1)
                act.activation(X[:, sl, :], X[:, sl, :], IDENT, bias=Bk[:, NBLK, b:b + 1]).then_inc(s["xb"], 1)

            def w0hi(q):
                st, k, b, sl = where(q * QS)
                act.wait_ge(s["bv1"], k + 1)
                act.wait_ge(s["w03"], k + 1)
                if q >= 2:
                    act.wait_ge(s["conv0"], QS * (q - 1))
                for i in range(QS):
                    ins = act.activation(w0h[q % 2][:, i, :], w0f[:, k, :, :].rearrange("p j c -> p (j c)"), ACT.Copy,
                                         scale=tab["S0"][:, k, b + i:b + i + 1])
                ins.then_inc(s["w0h"], 1)

            def w3hi(q):
                act.wait_ge(s["w3q"], q + 1)
                if q >= 1:
                    act.wait_ge(s["V"], q)
                act.activation(w3h[:, :, :, :], w3q[:, :, :, :], ACT.Copy).then_inc(s["w3h"], 1)

            def vhi(q):
                act.wait_ge(s["vf"], q + 1)
                if q >= 1:
                    act.wait_ge(s["G"], q)
                act.activation(vh[:, :, :, :], vf[:, :, :, :], ACT.Copy).then_inc(s["vh"], 1)

            def ghi(q):
                act.wait_ge(s["gp"], q + 1)
                for h in (2 * q, 2 * q + 1):
                    if h >= 3:
                        act.wait_ge(s["convg"], 2 * (h - 2))
                    act.activation(gh[h % 3][:, :, :, :], gp[:, 2 * (h % 2):2 * (h % 2) + 2, :, :], ACT.Copy).then_inc(s["gh"], 1)

            w3hi(0)
            for n in range(FIRST, NN):
                if 0 <= n + 1 < NN:
                    zhi(n + 1)
                if 0 <= n + 2 < NN:
                    xhi(n + 2)
                if g_at(n - 2) is not None:
                    ghi(g_at(n - 2))
                if v_at(n - 1) is not None:
                    vhi(v_at(n - 1))
                k, stages = setup_at(n)
                for stage in stages:
                    setup(k, stage)
                if v_at(n + 1) is not None and v_at(n + 1) > 0:
                    w3hi(v_at(n + 1))
                if g_at(n + 1) is not None:
                    w0hi(g_at(n + 1))
                if n >= 0 and where(n)[1] == NBLK - 1:
                    xb(n)
                if n >= 0 and loads_at(n) is not None:
                    xcopy(loads_at(n))
                for b in range(*FIRST_COPIES.get(n, (0,))):
                    xcopy(b)

        @block.vector
        def _(dve):
            chain = [0]

            def link(ins):
                chain[0] += 1
                ins.then_inc(s["dve_set"], 1)
                dve.wait_ge(s["dve_set"], chain[0])

            def bc(a, n):
                return a.unsqueeze(2).broadcast_to([a.shape[0], a.shape[1], n])

            fl = ps[:, EP:EP + 2, :].rearrange("p k n -> p (k n)")

            def setup(k, stage):
                T = {n: t[:, k, :] for n, t in tab.items()}
                mb, bi = vec[:, 4 * k:4 * k + 4], [vec[:, NL + 4 * k + l:NL + 4 * k + l + 1] for l in range(NLAY)]

                def ch(a):
                    return a.broadcast_to([128, NB])

                if stage == TRANSPOSE:
                    dve.wait_ge(s["wT"], k + 1)
                    w = wT[C:128, k, :, :, :]
                    dve.tensor_tensor(wsq[:, 0:3], w, w, ALU.mult)
                    link(dve.tensor_tensor(wsq[:, 3], w1T[C:128], w1T[C:128], ALU.mult))
                    link(dve.tensor_tensor(wsum, wsq[:, :, 0, :], wsq[:, :, 1, :], ALU.add))
                    link(dve.tensor_tensor(wsum, wsum, wsq[:, :, 2, :], ALU.add))
                elif stage == STYLE:
                    dve.wait_ge(s["Sp"], k + 1)
                    link(dve.tensor_tensor(sall, fl[:, 0:4 * NB].rearrange("p (l b) -> p l b", l=NLAY), bc(mb, NB), ALU.add))
                    dve.tensor_tensor(ssq, sall[C:128], sall[C:128], ALU.mult).then_inc(s["sq"], 1)
                elif stage == DEMOD:
                    dve.wait_ge(s["Dp"], k + 1)
                    dve.tensor_scalar(var, fl[:, 512:512 + 4 * NB].rearrange("p (l b) -> p l b", l=NLAY),
                                      SCALE * SCALE, EPS, ALU.mult, ALU.add).then_inc(s["var"], 1)
                    dve.wait_ge(s["var"], k + 1)
                    dve.reciprocal(tmp, var).then_inc(s["rcp"], 1)
                elif stage == NEWTON:
                    dve.wait_ge(s["sqrt"], k + 1)
                    link(dve.tensor_tensor(tmp, dall, dall, ALU.mult))
                    link(dve.tensor_tensor(tmp, tmp, var, ALU.mult))
                    link(dve.tensor_scalar(tmp, tmp, -0.5 * SCALE, 1.5 * SCALE, ALU.mult, ALU.add))
                    link(dve.tensor_tensor(dall, dall, tmp, ALU.mult))
                elif stage == TABLES:
                    dve.scalar_tensor_tensor(tmp[:, 0, :], var[:, 0, :], 1.0 / (SCALE * SCALE), dall[:, 0, :],
                                             ALU.mult, ALU.mult)
                    dve.tensor_copy(T["S0"], sall[:, 0, :])
                    dve.tensor_tensor(T["T1"], dall[:, 0, :], dall[:, 1, :], ALU.mult)
                    dve.tensor_tensor(T["E1"], sall[:, 2, :], sall[:, 1, :], ALU.mult)
                    dve.tensor_tensor(T["E2"], sall[:, 3, :], dall[:, 2, :], ALU.mult)
                    dve.tensor_copy(T["D3"], dall[:, 3, :])
                    dve.tensor_tensor(T["ub"], sall[:, 2, :], ch(bi[1]), ALU.mult)
                    link(dve.tensor_tensor(T["sbb"], sall[:, 3, :], ch(bi[2]), ALU.mult))
                    link(dve.tensor_tensor(T["bz"], tmp[:, 0, :], ch(bi[0]), ALU.mult))
                    dve.tensor_scalar(bv[:, 0, :], T["ub"][C:128], 2.0, None, ALU.mult).then_inc(s["bv1"], 1)
                elif stage in (R_TAP0, R_TAP1, R_TAP2):
                    t = stage - R_TAP0
                    w = w1T[:, t, :].unsqueeze(1).broadcast_to([128, NJ, C])
                    link(dve.tensor_tensor(rf[min(t, 1)], w, bc(coef.rearrange("p (j t) -> p j t", t=K)[:, :, t], C),
                                           ALU.mult))
                    if t:
                        link(dve.tensor_tensor(rf[0], rf[0], rf[1], ALU.add))
                elif stage == SPLIT_W2:
                    dve.wait_ge(s["w2h"], k + 1)
                    w = wnat[:, 4 * k + 2, :].rearrange("p (i t) -> p t i", t=K)
                    hi = w2h[0:C, k, 0:3].bitcast(F32)
                    dve.tensor_tensor(w2l[0:C, k, 0:3], w, hi, ALU.subtract)
                    dve.tensor_tensor(w2l[C:128, k, 1:4], w, hi, ALU.subtract).then_inc(s["w2l"], 1)
                elif stage == SPLIT_R:
                    link(dve.tensor_copy(rh[:, k, :, :], rf[0]))
                    for h in range(2):
                        dve.tensor_copy(rd[h * C:(h + 1) * C, k], rf[0][0:C, 1:NJ - 1])
                    dve.tensor_tensor(rl[:, k, :, :], rf[0], rh[:, k, :, :].bitcast(F32),
                                      ALU.subtract).then_inc(s["rt"], 1)
                elif stage == BIAS_U:
                    dve.wait_ge(s["bp1"], k + 1)
                    link(dve.tensor_tensor(bv[:, 1, :], fl[C:128, 0:NB], T["E2"][C:128], ALU.mult))
                    dve.tensor_tensor(bv[:, 1, :], bv[:, 1, :], T["sbb"][C:128], ALU.add).then_inc(s["bv2"], 1)
                elif stage == BIAS_S:
                    dve.wait_ge(s["bp2"], k + 1)
                    link(dve.tensor_tensor(T["c3"], fl[:, 512:512 + NB], T["D3"], ALU.mult))
                    link(dve.tensor_tensor(beta, T["c3"], ch(bi[3]), ALU.add))
                    link(dve.tensor_scalar(T["c3"], T["c3"], -1.0, None, ALU.mult))
                    dve.tensor_tensor(Bk[:, k + 1, :], Bk[:, k, :], beta, ALU.add).then_inc(s["tabs"], 1)

            link(dve.memset(Bk[:, 0, :], 0.0))
            dve.memset(gp[:, :, :, :], 0.0)
            dve.wait_ge(s["tr0"], 1)
            link(dve.tensor_copy(styleT, ps[:, 0, 0:NB]))
            dve.tensor_copy(vec, ps[:, 0, NB:NB + 2 * NL]).then_inc(s["vec"], 1)
            dve.wait_ge(s["vec"], 1)
            for stage in (TRANSPOSE, STYLE, DEMOD, NEWTON, TABLES, SPLIT_W2, R_TAP0, R_TAP1, R_TAP2, SPLIT_R):
                setup(0, stage)
            dve.wait_ge(s["z0"], 3)

            def xlo(n):
                st, k, b, sl = where(n)
                dve.wait_ge(s["xhi"], n + 1)
                dve.scalar_tensor_tensor(xl[n % 2][:, 0:XW], X[:, sl, :], Bk[:, k, b:b + 1],
                                         xh[n % 2][:, 0:XW].bitcast(F32), ALU.add, ALU.subtract).then_inc(s["xlo"], 1)

            def zlo(n):
                st, k, b, sl = where(n)
                dve.wait_ge(s["zhi"], n + 1)
                dve.scalar_tensor_tensor(zl[n % 2][:, ZPAD:ZPAD + M], ps[:, ZP + n % 2, :], tab["bz"][:, k, b:b + 1],
                                         zh[n % 2][:, ZPAD:ZPAD + M].bitcast(F32), ALU.add, ALU.subtract) \
                    .then_inc(s["zlo"], 1)

            def xnew(n):
                st, k, b, sl = where(n)
                dve.wait_ge(s["convg"], n + 1)
                dve.wait_ge(s["en"], st + 1)
                o = ps[:, OP + n % 2, :]
                if k < NBLK - 1:
                    dve.scalar_tensor_tensor(X[:, sl, 1:M], o[:, 1:M], tab["D3"][:, k, b:b + 1], X[:, sl, 1:M],
                                             ALU.mult, ALU.add).then_inc(s["xnew"], 1)
                    return
                dve.wait_ge(s["xb"], b + 1)
                j = b // 2
                if j >= 2:
                    dve.wait_ge(s_out[j % 2], 16 * (j // 2))
                t = ot[j % 2][(b % 2) * C:(b % 2 + 1) * C, :]
                dve.scalar_tensor_tensor(t[:, 3:L - 1:2], o[0:C, 2:M], tab["D3"][0:C, k, b:b + 1], X[0:C, sl, 2:M],
                                         ALU.mult, ALU.add)
                dve.scalar_tensor_tensor(t[:, 2:L - 2:2], o[C:128, 1:M - 1], tab["D3"][C:128, k, b:b + 1],
                                         X[C:128, sl, 1:M - 1], ALU.mult, ALU.add).then_inc(s["xnew"], 1)

            def vfull(q):
                st, k, b, sl = where(q * QS)
                dve.wait_ge(s["V"], q + 1)
                if q >= 1:
                    dve.wait_ge(s["vl"], q)
                e = tab["E1"][:, k, b:b + QS].unsqueeze(1).unsqueeze(3).broadcast_to([128, 3, QS, C])
                pv = ps[:, VG:VG + 2, :].rearrange("p k (o s c) -> p (k o) s c", s=QS, c=C)[:, 0:3]
                dve.tensor_tensor(vf[:, :, :, :], pv, e, ALU.mult).then_inc(s["vf"], 1)

            def vlo(q):
                dve.wait_ge(s["vh"], q + 1)
                hi = vh[:, :, :, :].bitcast(F32)
                dve.tensor_tensor(vh[C:128, 2], vf[0:C, 2], hi[0:C, 2], ALU.subtract)
                dve.tensor_tensor(vl[:, :, :, :], vf[:, 0:2], hi[:, 0:2], ALU.subtract).then_inc(s["vl"], 1)

            def gplace(q, part):
                st, k, b, sl = where(q * QS)
                if part == 0:
                    dve.wait_ge(s["G"], q + 1)
                    if q >= 1:
                        dve.wait_ge(s["gl"], 2 * q)
                pg = ps[:, VG:VG + 2, :].rearrange("p k (o s c) -> p s (k o) c", s=QS, c=C)
                for row in (0, 1):
                    if part == 0:
                        src, dst = pg[0:C], gp[row * C:row * C + C, :, row:8:2, :]
                        t1, ns = tab["T1"][0:C, k, b:b + QS], 4
                    else:
                        src, dst = pg[C:128, :, 1:4], gp[row * C:row * C + C, :, 1 + row:6 + row:2, :]
                        t1, ns = tab["T1"][C:128, k, b:b + QS], 3
                    t1 = t1.unsqueeze(2).unsqueeze(3).broadcast_to([C, QS, ns, C])
                    ins = dve.tensor_tensor(dst, src, t1, ALU.mult)
                if part == 1:
                    ins.then_inc(s["gp"], 1)

            def w0lo(q):
                st, k, b, sl = where(q * QS)
                dve.wait_ge(s["w0h"], q + 1)
                for i in range(QS):
                    ins = dve.scalar_tensor_tensor(w0l[q % 2][:, i, :], w0f[:, k, :, :].rearrange("p j c -> p (j c)"),
                                                   tab["S0"][:, k, b + i:b + i + 1], w0h[q % 2][:, i, :].bitcast(F32),
                                                   ALU.mult, ALU.subtract)
                ins.then_inc(s["w0l"], 1)

            def glo0():
                for h in range(2):
                    dve.wait_ge(s["gh"], h + 1)
                    dve.tensor_tensor(gl[h][:, :, :, :], gp[:, 2 * h:2 * h + 2, :, :], gh[h][:, :, :, :].bitcast(F32),
                                      ALU.subtract).then_inc(s["gl"], 1)

            def edge(st, stage):
                g, k = STEPS[st]
                b = g * GS
                base = ps[0:C, EP + stage % 2, :]

                def t(name, n):
                    return tab[name][0:C, k, b:b + GS].unsqueeze(2).unsqueeze(3).broadcast_to([C, GS, 2, n])

                if stage == 0:
                    dve.wait_ge(s["zE"], st + 1)
                    dve.tensor_tensor(ze[:, :, :, 1:6], base[:, 0:GS * 10].rearrange("p (s e t) -> p s e t", s=GS, e=2),
                                      t("bz", 5), ALU.add).then_inc(s["zv"], 1)
                elif stage == 1:
                    dve.wait_ge(s["uE"], st + 1)
                    dve.tensor_tensor(ue[:, :, :, 1:12:2], base[:, 0:GS * 12].rearrange("p (s e t) -> p s e t", s=GS, e=2),
                                      t("E1", 6), ALU.mult)
                    dve.tensor_tensor(ue[:, :, :, 2:12:2], base[:, GS * 12:GS * 22].rearrange("p (s e t) -> p s e t", s=GS, e=2),
                                      t("E1", 5), ALU.mult).then_inc(s["uv"], 1)
                elif stage == 2:
                    dve.wait_ge(s["sE"], st + 1)
                    sv_ = base[:, 0:GS * 12].rearrange("p (s e t) -> p s e t", s=GS, e=2)
                    for e in range(2):
                        ins = dve.scalar_tensor_tensor(se[:, :, e, 2 - 2 * e:8 - 2 * e], sv_[:, :, e, :], 0.25,
                                                       tab["E2"][0:C, k, b:b + GS].unsqueeze(2).broadcast_to([C, GS, 6]),
                                                       ALU.mult, ALU.mult)
                    ins.then_inc(s["sv"], 1)
                else:
                    dve.wait_ge(s["oE"], st + 1)
                    o = ps[:, EP + 1, 0:GS * 4].rearrange("p (s t) -> p s t", s=GS)
                    dve.scalar_tensor_tensor(oe[:, :, :, :].rearrange("p s e t -> p s (e t)"), o, 0.125,
                                             tab["D3"][:, k, b:b + GS].unsqueeze(2).broadcast_to([128, GS, 4]),
                                             ALU.mult, ALU.mult) \
                        .then_inc(s["ov"], 1)

            for n in range(FIRST, NN):
                if n >= 1:
                    xnew(n - 1)
                if 0 <= n + 2 < NN:
                    xlo(n + 2)
                if 0 <= n + 1 < NN:
                    zlo(n + 1)
                if v_at(n - 1) is not None:
                    vlo(v_at(n - 1))
                k, stages = setup_at(n)
                for stage in stages:
                    setup(k, stage)
                if n >= -2 and edge_at(n)[0] is not None:
                    edge(*edge_at(n))
                if n == -2:
                    glo0()
                if v_at(n) is not None:
                    vfull(v_at(n))
                for part in range(2):
                    if g_at(n - part) is not None:
                        gplace(g_at(n - part), part)
                if n < -2 and edge_at(n)[0] is not None:
                    edge(*edge_at(n))
                if g_at(n + 1) is not None:
                    w0lo(g_at(n + 1))
            xnew(NN - 1)

        @block.gpsimd
        def _(pool):
            counts, open_ = {"gl": 2}, {}

            def sig(ins, name="chp", by=1):
                ins.then_inc(s[name], by)
                counts[name] = open_[name] = counts.get(name, 0) + by

            def fence():
                for name, n in open_.items():
                    pool.wait_ge(s[name], n)
                open_.clear()

            def link(ins):
                sig(ins)
                fence()

            for r in raw:
                sig(pool.memset(r[0:C, 0:1], 0.0))
                sig(pool.memset(r[0:C, L + 1:L + 2], 0.0))
                fence()
                link(pool.memset(r[C:128, L:L + 2], 0.0))
            for a in (xe, ze, ue, ye, se):
                link(pool.memset(a[:, :, :, :], 0.0))
            sig(pool.memset(w0f[:, :, :, :], 0.0), "z0")
            for a in (w2h, w2l):
                link(pool.memset(a[0:C, :, 3].bitcast(F32), 0.0))
                link(pool.memset(a[C:128, :, 0].bitcast(F32), 0.0))
            sig(pool.memset(w2d[:, :, 3].bitcast(F32), 0.0), "z0")
            for a in (zh[0], zh[1], zl[0], zl[1]):
                link(pool.memset(a[:, :].bitcast(F32), 0.0))
            sig(pool.memset(en[:, :, :, :], 0.0), "z0")

            def w3s(q):
                st, k, b, sl = where(q * QS)
                pool.wait_ge(s["bv1"], k + 1)
                pool.wait_ge(s["w03"], k + 1)
                if q >= 1:
                    pool.wait_ge(s["V"], q)
                e = tab["E2"][:, k, b:b + QS].unsqueeze(1).unsqueeze(3).broadcast_to([128, 2, QS, C])
                w = w3f[:, k, :, :].unsqueeze(2).broadcast_to([128, 2, QS, C])
                sig(pool.tensor_tensor(w3q[:, :, :, :], w, e, ALU.mult), "w3q")

            def w3lo(q):
                pool.wait_ge(s["w3h"], q + 1)
                fence()
                hi = w3h[:, :, :, :].bitcast(F32)
                link(pool.tensor_tensor(w3h[C:128, 1], w3q[C:128, 1], hi[C:128, 1], ALU.subtract))
                sig(pool.tensor_tensor(w3l[:, :, :], w3q[:, 0], hi[:, 0], ALU.subtract), "w3l")

            def glo(q):
                if q == 0:
                    return
                for h in (2 * q, 2 * q + 1):
                    pool.wait_ge(s["gh"], h + 1)
                    sig(pool.tensor_tensor(gl[h % 3][:, :, :, :], gp[:, 2 * (h % 2):2 * (h % 2) + 2, :, :],
                                           gh[h % 3][:, :, :, :].bitcast(F32),
                                           ALU.subtract), "gl")

            def x_ends(st):
                g, k = STEPS[st]
                return X[:, (g % NR) * GS:(g % NR + 1) * GS, :]

            def edge_x(st):
                g, k = STEPS[st]
                b = g * GS
                if k == 0:
                    pool.wait_ge(s["xcopy"], b + GS)
                else:
                    pool.wait_ge(s["xnew"], GS * (st - 1))
                    pool.wait_ge(s["eap"], st - 1)
                if st >= 1:
                    pool.wait_ge(s["zE"], st)
                xv = x_ends(st)
                for e in range(2):
                    lo, hi = (slice(1, 4), slice(0, 3)) if e == 0 else (slice(M - 2, M + 1), slice(M - 3, M))
                    at = 1 - e
                    sig(pool.tensor_tensor(xe[:, :, e, at + 1:at + 6:2], xv[0:C, :, lo],
                                       Bk[0:C, k, b:b + GS].unsqueeze(2).broadcast_to([C, GS, 3]), ALU.add))
                    fence()
                    link(pool.tensor_tensor(xe[:, :, e, at:at + 5:2], xv[C:128, :, hi],
                                            Bk[C:128, k, b:b + GS].unsqueeze(2).broadcast_to([C, GS, 3]), ALU.add))
                xf = xe[:, :, :, :].rearrange("p s e t -> p s (e t)")
                sig(pool.tensor_tensor(xf, xf, tab["S0"][0:C, k, b:b + GS].unsqueeze(2).broadcast_to([C, GS, 14]),
                                   ALU.mult), "xe")

            def edge_z(st):
                g, k = STEPS[st]
                b = g * GS
                pool.wait_ge(s["zv"], st + 1)
                zf = ze[:, :, :, :].rearrange("p s e t -> p s (e t)")
                sig(pool.tensor_tensor(zf, zf, tab["T1"][0:C, k, b:b + GS].unsqueeze(2).broadcast_to([C, GS, 14]),
                                   ALU.mult), "ze")

            def blur(dst, src, n, off, last, name):
                a1, a2 = b1[:, :, :, 0:n + 2], b2[:, :, :, 0:n + 1]
                for e in range(2):
                    o = off[e]
                    ins = pool.tensor_tensor(a1[:, :, e, :], src[:, :, e, o:o + n + 2], src[:, :, e, o + 1:o + n + 3], ALU.add)
                    sig(ins)
                fence()
                link(pool.tensor_tensor(a2, b1[:, :, :, 0:n + 1], b1[:, :, :, 1:n + 2], ALU.add))
                for e in range(2):
                    o = last[e]
                    ins = pool.tensor_tensor(dst[:, :, e, o:o + n], b2[:, :, e, 0:n], b2[:, :, e, 1:n + 1], ALU.add)
                    sig(ins, name if e else "chp")

            def edge_u(st):
                g, k = STEPS[st]
                b = g * GS
                pool.wait_ge(s["uv"], st + 1)
                uv = ue[:, :, :, 1:12]
                link(pool.tensor_tensor(uv, uv, tab["ub"][0:C, k, b:b + GS].unsqueeze(2).unsqueeze(3)
                                        .broadcast_to([C, GS, 2, 11]), ALU.add))
                blur(ye, ue, 7, (0, 3), (1, 0), "ye")

            def edge_s(st):
                g, k = STEPS[st]
                b = g * GS
                pool.wait_ge(s["sv"], st + 1)
                for e in range(2):
                    sv_ = se[:, :, e, 2 - 2 * e:8 - 2 * e]
                    ins = pool.tensor_tensor(sv_, sv_, tab["sbb"][0:C, k, b:b + GS].unsqueeze(2).broadcast_to([C, GS, 6]), ALU.add)
                    sig(ins)
                fence()
                blur(ve, se, 5, (0, 0), (0, 0), "ve")

            def edge_o(st):
                g, k = STEPS[st]
                b = g * GS
                xv = x_ends(st)
                pool.wait_ge(s["ov"], st + 1)
                of = oe[:, :, :, :].rearrange("p s e t -> p s (e t)")
                link(pool.tensor_tensor(of, of, tab["c3"][:, k, b:b + GS].unsqueeze(2).broadcast_to([128, GS, 4]), ALU.add))
                ev = en[:, st % 2, :, :]
                sig(pool.tensor_tensor(ev[0:C], oe[0:C, :, :, 1], xv[0:C, :, 1:M + 1:M - 1], ALU.add))
                fence()
                ins = pool.tensor_tensor(ev[C:128], oe[C:128, :, :, 0], xv[C:128, :, 0:M:M - 1], ALU.add)
                if k == NBLK - 1:
                    link(ins)
                    ins = pool.tensor_tensor(ev, ev, Bk[:, NBLK, b:b + GS].unsqueeze(2).broadcast_to([128, GS, 2]), ALU.add)
                sig(ins, "en")
                fence()

            def edge_apply(st):
                g, k = STEPS[st]
                b = g * GS
                pool.wait_ge(s["xnew"], GS * (st + 1))
                xv, ev = x_ends(st), en[:, st % 2, :, :]
                fence()
                if k < NBLK - 1:
                    link(pool.tensor_copy(xv[C:128, :, 0:M:M - 1], ev[C:128]))
                    link(pool.tensor_scalar(xv[C:128, :, M], Bk[C:128, k + 1, b:b + GS], -1.0, None, ALU.mult))
                    sig(pool.tensor_copy(xv[0:C, :, 1:M + 1:M - 1], ev[0:C]))
                    sig(pool.tensor_scalar(xv[0:C, :, 0], Bk[0:C, k + 1, b:b + GS], -1.0, None, ALU.mult), "eap")
                else:
                    sig(pool.memset(b1[:, 0, 0, 0:1], 0.0), "eap")
                fence()

            def finish(n):
                st, k, b, sl = where(n)
                pool.wait_ge(s["en"], st + 1)
                j = b // 2
                if j >= 2:
                    pool.wait_ge(s_out[j % 2], 16 * (j // 2))
                t = ot[j % 2][(b % 2) * C:(b % 2 + 1) * C, :]
                ev = en[:, st % 2, b % GS, :]
                fence()
                link(pool.tensor_copy(t[:, 0:L - 1:L - 2], ev[C:128]))
                sig(pool.tensor_copy(t[:, 1:L:L - 2], ev[0:C]), "oed")
                fence()

            w3s(0)
            w3lo(0)
            for n in range(FIRST, NN):
                st, i = divmod(n, GS)
                if n >= 0:
                    if STEPS[st][1] == NBLK - 1:
                        finish(n)
                if n < 0:
                    for at, stage in ((-5, edge_x), (-4, edge_z), (-3, edge_u), (-2, edge_s), (-1, edge_o)):
                        if n == at:
                            stage(0)
                if n >= 1 and n % GS == 1 and st >= 1:
                    edge_apply(st - 1)
                if n >= 0 and st + 1 < NS:
                    for at, stage in ((2, edge_x), (3, edge_z), (4, edge_u), (6, edge_s), (7, edge_o)):
                        if i == at:
                            stage(st + 1)
                if g_at(n - 2) is not None:
                    glo(g_at(n - 2))
                if v_at(n + 1) is not None and v_at(n + 1) > 0:
                    w3lo(v_at(n + 1))
                if v_at(n + 2) is not None and v_at(n + 2) > 0:
                    w3s(v_at(n + 2))


def kernel(**inputs):
    import concourse.bacc as bacc
    from concourse.bass_utils import run_bass_kernel_spmd

    nc = bacc.Bacc("TRN2", target_bir_lowering=False, num_devices=1)
    arrays = {}

    def dram(name, a):
        a = np.ascontiguousarray(a)
        arrays[name] = a
        return nc.dram_tensor(name, a.shape, mybir.dt.from_np(a.dtype), kind="ExternalInput").ap()

    x = dram("x_in", inputs["x"])
    style = dram("style_in", inputs["cond_512"])
    weights, biases, mod_w, mod_b = (
        [dram(f"{what}{k}_in", inputs[f"L{k}_cond_{what}"]) for k in range(NBLK)]
        for what in ("weights", "biases", "mod_w", "mod_b"))
    ident_d = dram("ident_in", np.eye(128, dtype=np.float32))
    coef_d = dram("coef_in", blur_table())
    out = nc.dram_tensor("out_x", (NB, C, L), F32, kind="ExternalOutput").ap()
    build(nc, x, style, weights, biases, mod_w, mod_b, ident_d, coef_d, out)
    r = run_bass_kernel_spmd(nc, [arrays], core_ids=[0])
    return r.results[0]["out_x"]
```
